# Optimizing a Trainium2 kernel written in Bass

```python
import numpy as np
import jax
import jax.numpy as jnp

def _softmax(x, axis=-1):
    return jax.nn.softmax(x, axis=axis)

def _gelu(x):
    return jax.nn.gelu(x, approximate=True)

def _silu(x):
    return jax.nn.silu(x)

def _sigmoid(x):
    return jax.nn.sigmoid(x)

def _layernorm(x, axis=-1, eps=1e-05):
    m = jnp.mean(x, axis=axis, keepdims=True)
    v = jnp.var(x, axis=axis, keepdims=True)
    return (x - m) / jnp.sqrt(v + eps)

def _scatter_add(tgt, idx, src, axis=0):
    return tgt.at[idx].add(src)

def _segment_sum(src, seg, n):
    return jax.ops.segment_sum(src, seg, n)
kernel_name = 'mk_cond_resid_d4_seqx_r2_b9a6c9'

def setup_inputs(seed: int=0):
    np.random.seed(seed)
    _w = jnp.asarray

    def _rec_inputs():
        import jax
        import jax.numpy as jnp
        _rk = jax.random.key(seed)
        x = -0.000125 + 0.9999 * jax.random.normal(jax.random.fold_in(_rk, 1), (128, 128, 2048), jnp.float32)
        _lenS = 128 - jax.random.randint(jax.random.fold_in(_rk, 7), (128,), 0, max(1, 128 // 4) + 1, jnp.int32)
        _lenS2 = 128 - jax.random.randint(jax.random.fold_in(_rk, 8), (128,), 0, max(1, 128 // 4) + 1, jnp.int32)
        cond_128 = 0.0061147 + 1.02565 * jax.random.normal(jax.random.fold_in(_rk, 11), (128, 128), jnp.float32)
        fside_S_0 = -0.022604 + 0.987366 * jax.random.normal(jax.random.fold_in(_rk, 12), (128,), jnp.float32)
        return (x, cond_128, fside_S_0)
    x, cond_128, fside_S_0 = _rec_inputs()

    def _L0_cond_setup():
        import jax, jax.numpy as jnp
        import numpy as np
        from jax import lax
        N, C_IN, L = (32, 128, 2048)
        C_OUT, K, GROUPS = (128, 9, 4)
        C_DIM, PAD, STRIDE = (128, 4, 1)
        key = jax.random.key(seed)
        k1, k2, k3, k4, k5 = jax.random.split(key, 5)
        x = jax.random.normal(k1, (N, C_IN, L), dtype=jnp.float32)
        c = jax.random.normal(k2, (N, C_DIM), dtype=jnp.float32)
        weight = jax.random.normal(k3, (C_OUT, C_IN // GROUPS, K), dtype=jnp.float32)
        c_weight = jax.random.normal(k4, (C_OUT, C_DIM), dtype=jnp.float32)
        bias = jax.random.normal(k5, (C_OUT,), dtype=jnp.float32)
        return {'x': x, 'c': c, 'weight': weight, 'c_weight': c_weight, 'bias': bias}
    _L0_cond_all = _L0_cond_setup()
    _L0_cond_in = {k: v for k, v in _L0_cond_all.items() if k in ('weight', 'c_weight')}
    del _L0_cond_all

    def _L1_cond_setup():
        import jax, jax.numpy as jnp
        import numpy as np
        K = 8
        T = 1.0
        D_EMBD = 128
        IN_C = 128
        OUT_C = 128
        BS = 32
        H = 2048
        HID = 128
        key = jax.random.key(seed)
        ks = jax.random.split(key, 10)
        s = lambda fan_in: 1.0 / np.sqrt(fan_in)
        return {'x': jax.random.normal(ks[0], (BS, IN_C, H), dtype=jnp.float32), 'embedding': jax.random.normal(ks[1], (BS, D_EMBD), dtype=jnp.float32), 'W0': jax.random.normal(ks[2], (D_EMBD, HID), dtype=jnp.float32) * s(D_EMBD), 'b0': jnp.zeros((HID,), dtype=jnp.float32), 'W1': jax.random.normal(ks[3], (HID, HID), dtype=jnp.float32) * s(HID), 'b1': jnp.zeros((HID,), dtype=jnp.float32), 'W2': jax.random.normal(ks[4], (HID, K), dtype=jnp.float32) * s(HID), 'b2': jnp.zeros((K,), dtype=jnp.float32), 'weight': jax.random.normal(ks[5], (K, OUT_C, IN_C, 1), dtype=jnp.float32) * s(IN_C), 'bias_k': jax.random.normal(ks[6], (K, OUT_C), dtype=jnp.float32) * 0.1}
    _L1_cond_all = _L1_cond_setup()
    _L1_cond_in = {k: v for k, v in _L1_cond_all.items() if k in ('W0', 'b0', 'W1', 'b1', 'W2', 'b2', 'weight', 'bias_k')}
    del _L1_cond_all

    def _L2_cond_setup():
        import jax, jax.numpy as jnp
        import numpy as np
        K = 8
        T = 1.0
        D_EMBD = 128
        IN_C = 128
        OUT_C = 128
        BS = 32
        H = 2048
        HID = 128
        key = jax.random.key(seed)
        ks = jax.random.split(key, 10)
        s = lambda fan_in: 1.0 / np.sqrt(fan_in)
        return {'x': jax.random.normal(ks[0], (BS, IN_C, H), dtype=jnp.float32), 'embedding': jax.random.normal(ks[1], (BS, D_EMBD), dtype=jnp.float32), 'W0': jax.random.normal(ks[2], (D_EMBD, HID), dtype=jnp.float32) * s(D_EMBD), 'b0': jnp.zeros((HID,), dtype=jnp.float32), 'W1': jax.random.normal(ks[3], (HID, HID), dtype=jnp.float32) * s(HID), 'b1': jnp.zeros((HID,), dtype=jnp.float32), 'W2': jax.random.normal(ks[4], (HID, K), dtype=jnp.float32) * s(HID), 'b2': jnp.zeros((K,), dtype=jnp.float32), 'weight': jax.random.normal(ks[5], (K, OUT_C, IN_C, 1), dtype=jnp.float32) * s(IN_C), 'bias_k': jax.random.normal(ks[6], (K, OUT_C), dtype=jnp.float32) * 0.1}
    _L2_cond_all = _L2_cond_setup()
    _L2_cond_in = {k: v for k, v in _L2_cond_all.items() if k in ('W0', 'b0', 'W1', 'b1', 'W2', 'b2', 'weight', 'bias_k')}
    del _L2_cond_all

    def _L3_cond_setup():
        import jax, jax.numpy as jnp
        import numpy as np
        from jax import lax
        N, C_IN, L = (32, 128, 2048)
        C_OUT, K, GROUPS = (128, 9, 4)
        C_DIM, PAD, STRIDE = (128, 4, 1)
        key = jax.random.key(seed)
        k1, k2, k3, k4, k5 = jax.random.split(key, 5)
        x = jax.random.normal(k1, (N, C_IN, L), dtype=jnp.float32)
        c = jax.random.normal(k2, (N, C_DIM), dtype=jnp.float32)
        weight = jax.random.normal(k3, (C_OUT, C_IN // GROUPS, K), dtype=jnp.float32)
        c_weight = jax.random.normal(k4, (C_OUT, C_DIM), dtype=jnp.float32)
        bias = jax.random.normal(k5, (C_OUT,), dtype=jnp.float32)
        return {'x': x, 'c': c, 'weight': weight, 'c_weight': c_weight, 'bias': bias}
    _L3_cond_all = _L3_cond_setup()
    _L3_cond_in = {k: v for k, v in _L3_cond_all.items() if k in ('weight', 'c_weight')}
    del _L3_cond_all
    return {'x': x, 'cond_128': cond_128, 'fside_S_0': fside_S_0, 'L0_cond_weight': _L0_cond_in['weight'], 'L0_cond_c_weight': _L0_cond_in['c_weight'], 'L1_cond_W0': _L1_cond_in['W0'], 'L1_cond_b0': _L1_cond_in['b0'], 'L1_cond_W1': _L1_cond_in['W1'], 'L1_cond_b1': _L1_cond_in['b1'], 'L1_cond_W2': _L1_cond_in['W2'], 'L1_cond_b2': _L1_cond_in['b2'], 'L1_cond_weight': _L1_cond_in['weight'], 'L1_cond_bias_k': _L1_cond_in['bias_k'], 'L2_cond_W0': _L2_cond_in['W0'], 'L2_cond_b0': _L2_cond_in['b0'], 'L2_cond_W1': _L2_cond_in['W1'], 'L2_cond_b1': _L2_cond_in['b1'], 'L2_cond_W2': _L2_cond_in['W2'], 'L2_cond_b2': _L2_cond_in['b2'], 'L2_cond_weight': _L2_cond_in['weight'], 'L2_cond_bias_k': _L2_cond_in['bias_k'], 'L3_cond_weight': _L3_cond_in['weight'], 'L3_cond_c_weight': _L3_cond_in['c_weight']}

def reference(x, cond_128, fside_S_0, L0_cond_weight, L0_cond_c_weight, L1_cond_W0, L1_cond_b0, L1_cond_W1, L1_cond_b1, L1_cond_W2, L1_cond_b2, L1_cond_weight, L1_cond_bias_k, L2_cond_W0, L2_cond_b0, L2_cond_W1, L2_cond_b1, L2_cond_W2, L2_cond_b2, L2_cond_weight, L2_cond_bias_k, L3_cond_weight, L3_cond_c_weight):
    import jax
    import jax.numpy as jnp

    def _L0_cond_ref(x, c, weight, c_weight, bias):
        import jax, jax.numpy as jnp
        import numpy as np
        from jax import lax
        N, C_IN, L = (32, 128, 2048)
        C_OUT, K, GROUPS = (128, 9, 4)
        C_DIM, PAD, STRIDE = (128, 4, 1)
        out = lax.conv_general_dilated(x, weight, window_strides=(STRIDE,), padding=[(PAD, PAD)], dimension_numbers=('NCH', 'OIH', 'NCH'), feature_group_count=GROUPS)
        ctx = jnp.einsum('nd,od->no', c, c_weight)
        out = out + ctx[:, :, None] + bias[None, :, None]
        return out

    def _L1_cond_ref(x, embedding, W0, b0, W1, b1, W2, b2, weight, bias_k):
        import jax, jax.numpy as jnp
        import numpy as np
        K = 8
        T = 1.0
        D_EMBD = 128
        IN_C = 128
        OUT_C = 128
        BS = 32
        H = 2048
        HID = 128
        h = jax.nn.gelu(embedding @ W0 + b0, approximate=False)
        h = jax.nn.gelu(h @ W1 + b1, approximate=False)
        att = jax.nn.softmax((h @ W2 + b2) / T, axis=-1)
        agg_w = jnp.einsum('bk,koi->boi', att, weight[..., 0])
        agg_b = att @ bias_k
        out = jnp.einsum('boi,bih->boh', agg_w, x) + agg_b[:, :, None]
        return out

    def _L2_cond_ref(x, embedding, W0, b0, W1, b1, W2, b2, weight, bias_k):
        import jax, jax.numpy as jnp
        import numpy as np
        K = 8
        T = 1.0
        D_EMBD = 128
        IN_C = 128
        OUT_C = 128
        BS = 32
        H = 2048
        HID = 128
        h = jax.nn.gelu(embedding @ W0 + b0, approximate=False)
        h = jax.nn.gelu(h @ W1 + b1, approximate=False)
        att = jax.nn.softmax((h @ W2 + b2) / T, axis=-1)
        agg_w = jnp.einsum('bk,koi->boi', att, weight[..., 0])
        agg_b = att @ bias_k
        out = jnp.einsum('boi,bih->boh', agg_w, x) + agg_b[:, :, None]
        return out

    def _L3_cond_ref(x, c, weight, c_weight, bias):
        import jax, jax.numpy as jnp
        import numpy as np
        from jax import lax
        N, C_IN, L = (32, 128, 2048)
        C_OUT, K, GROUPS = (128, 9, 4)
        C_DIM, PAD, STRIDE = (128, 4, 1)
        out = lax.conv_general_dilated(x, weight, window_strides=(STRIDE,), padding=[(PAD, PAD)], dimension_numbers=('NCH', 'OIH', 'NCH'), feature_group_count=GROUPS)
        ctx = jnp.einsum('nd,od->no', c, c_weight)
        out = out + ctx[:, :, None] + bias[None, :, None]
        return out
    x = x + _L0_cond_ref(x, cond_128, L0_cond_weight, L0_cond_c_weight, fside_S_0)
    x = x + _L1_cond_ref(x, cond_128, L1_cond_W0, L1_cond_b0, L1_cond_W1, L1_cond_b1, L1_cond_W2, L1_cond_b2, L1_cond_weight, L1_cond_bias_k)
    x = x + _L2_cond_ref(x, cond_128, L2_cond_W0, L2_cond_b0, L2_cond_W1, L2_cond_b1, L2_cond_W2, L2_cond_b2, L2_cond_weight, L2_cond_bias_k)
    x = x + _L3_cond_ref(x, cond_128, L3_cond_weight, L3_cond_c_weight, fside_S_0)
    return x

_drawn_inputs = setup_inputs


def setup_inputs(seed=0):
    import zlib

    import numpy as np

    out = dict(_drawn_inputs(seed))
    spreads = {'L1_cond_b0': (0.0, 0.68),
     'L1_cond_b1': (0.0, 0.482),
     'L1_cond_b2': (0.0, 0.386),
     'L2_cond_b0': (0.0, 0.649),
     'L2_cond_b1': (0.0, 0.356),
     'L2_cond_b2': (0.0, 0.436)}
    factors = {'L1_cond_bias_k': 37.812, 'L2_cond_bias_k': 40.559}
    for name, (base, spread) in spreads.items():
        noise = np.random.default_rng([zlib.crc32(name.encode()), seed]).standard_normal(out[name].shape)
        drawn = base * np.exp(spread * noise) if base else spread * noise
        out[name] = jnp.asarray(drawn.astype(out[name].dtype))
    for name, factor in factors.items():
        out[name] = (out[name] * factor).astype(out[name].dtype)
    return out
```

```python
import concourse.bass as bass
from concourse import mybir
from contextlib import ExitStack


def cond_resid_kernel(nc: bass.Bass, a, out):
    f32, f32r = mybir.dt.float32, mybir.dt.float32r
    ALU, ACT, AX = mybir.AluOpType, mybir.ActivationFunctionType, mybir.AxisListType

    B, C, L = a["x"].shape
    GROUP = a["W0"].shape[0]
    TAPS = a["W0"].shape[1] // C
    G = C // GROUP
    PH = C // GROUP
    N = L // PH
    BLK = (PH + TAPS - 1) // PH
    HALO = BLK // 2
    K = a["e0"].shape[0]
    KI = K + 1
    DMA = 16
    ODD = 2

    ctx = ExitStack()
    with ctx:
        def sb(name, shape, dt=f32):
            return ctx.enter_context(nc.sbuf_tensor(name, shape, dt))

        def sem(name):
            return ctx.enter_context(nc.semaphore(name))

        x_in = sb("x_in", [C, ODD, L])
        x_ch = sb("x_ch", [C, PH, N])
        x_ph = sb("x_ph", [C, G, N])
        x_hi = sb("x_hi", [C, G, N + 2 * HALO], f32r)
        x_lo = sb("x_lo", [C, G, N + 2 * HALO], f32r)
        x1_ph = sb("x1_ph", [C, G, N])
        x1_ch = sb("x1_ch", [C, PH, N])
        x3_hi = sb("x3_hi", [C, G, N + 2 * HALO], f32r)
        x3_lo = sb("x3_lo", [C, G, N + 2 * HALO], f32r)
        x4_ph = sb("x4_ph", [C, G, N])
        x4_ch = sb("x4_ch", [C, PH, N])
        x_out = sb("x_out", [C, ODD, L])
        band = [sb(f"band{l}", [C, BLK, PH, G, GROUP]) for l in range(2)]
        w_hi = [sb(f"w_hi{l}", [C, BLK, G, C], f32r) for l in range(2)]
        w_lo = [sb(f"w_lo{l}", [C, BLK, G, C], f32r) for l in range(2)]
        expert = [sb(f"expert{l}", [C, KI, C]) for l in range(2)]
        mix = [sb(f"mix{l}", [C, B, KI]) for l in range(2)]
        weighted = sb("weighted", [C, KI, C])
        mixed = [sb(f"mixed{l}", [C, C]) for l in range(2)]
        m_t = sb("m_t", [C, C])
        bias1 = sb("bias1", [C, B])
        bias_l = [sb(f"bias_l{l}", [C, B]) for l in range(2)]
        bias4_ch = sb("bias4_ch", [C, B])
        bias4 = sb("bias4", [C, G, B])
        vec_g = sb("vec_g", [C, G])
        bias3_now = sb("bias3_now", [C, G])
        bias4_now = sb("bias4_now", [C, G])
        ident = sb("ident", [C, C])
        ones = sb("ones", [C, C])
        in_rank = sb("in_rank", [C, GROUP])
        spread_qc = sb("spread_qc", [C, PH, GROUP])
        spread_cq = sb("spread_cq", [C, GROUP, PH])
        in_group = sb("in_group", [C, G])
        cond_t = sb("cond_t", [C, B])
        side = sb("side", [C, 1])
        cw = [sb(f"cw{l}", [C, C]) for l in range(2)]
        w0 = [sb(f"w0_{l}", [C, C]) for l in range(2)]
        w1 = [sb(f"w1_{l}", [C, C]) for l in range(2)]
        w2 = [sb(f"w2_{l}", [C, K]) for l in range(2)]
        b0 = [sb(f"b0_{l}", [C, 1]) for l in range(2)]
        b1 = [sb(f"b1_{l}", [C, 1]) for l in range(2)]
        b2 = [sb(f"b2_{l}", [1, K]) for l in range(2)]
        bias_k = [sb(f"bias_k{l}", [K, C]) for l in range(2)]
        h1 = [sb(f"h1_{l}", [C, B]) for l in range(2)]
        h2 = [sb(f"h2_{l}", [C, B]) for l in range(2)]
        top = [sb(f"top{l}", [B, 1]) for l in range(2)]
        total = [sb(f"total{l}", [B, 1]) for l in range(2)]
        share = [sb(f"share{l}", [B, 1]) for l in range(2)]
        att = [sb(f"att{l}", [B, KI]) for l in range(2)]
        att_t = [sb(f"att_t{l}", [K, B]) for l in range(2)]
        att_diag = [t.rearrange("p g n -> p (g n)")[:, 0:B * KI] for t in (x1_ch[0:B, :, :], x4_ch[0:B, :, :])]
        bias4_g = x4_ph[:, 0, 0:G * B].rearrange("p (g b) -> p g b", g=G)

        bank = [ctx.enter_context(nc.psum_tensor(f"bank{n}", [C, N], f32)) for n in range(8)]
        conv_bank = bank[0:2]
        mid_bank = bank[2:2 + G]
        prep = bank[6]
        m_ps, v_ps, b_ps = prep[:, 0:C], prep[:, C:C + 1], prep[:, C + 4:C + 4 + G]

        s_in = sem("setup_loaded")
        taps_placed = [sem(f"conv_taps_placed{l}") for l in range(2)]
        zeroed = sem("ident_ones_halos_filled")
        ident_ready = sem("identity_ready")
        h1_done = sem("hidden1_in_psum")
        h1_ready = sem("hidden1_in_sbuf")
        h2_done = sem("hidden2_in_psum")
        h2_ready = sem("hidden2_in_sbuf")
        score_done = sem("scores_in_psum")
        top_ready = sem("score_maximum_negated")
        exp_ready = sem("exponentials_ready")
        share_ready = sem("one_over_their_sum")
        att_ready = sem("attention_ready")
        diag_ready = sem("attention_on_diagonal")
        att_t_done = sem("attention_transposed_in_psum")
        att_t_ready = sem("attention_transposed_in_sbuf")
        mix_done = sem("mix_third_in_psum")
        mix_copied = sem("mix_third_in_sbuf")
        bias_l_done = sem("layer_bias_in_psum")
        bias_l_ready = sem("layer_bias_in_sbuf")
        ctx_done = sem("context_in_psum")
        ctx_ready = sem("context_bias_in_sbuf")
        masks_ready = sem("spread_and_group_masks")
        bias4_g_ready = sem("bias4_masked_by_group")
        bias4_done = sem("bias4_in_psum")
        bias4_all = sem("bias4_in_sbuf")
        eye_ready = sem("identity_expert_written")
        band_zeroed = sem("band_zeroed")
        band_ready = sem("band_with_residual")
        w_hi_ready = sem("conv_weights_high")
        w_lo_ready = sem("conv_weights_low")
        weighted_ready = sem("experts_weighted")
        x_loaded = [sem(f"x_loaded{n}") for n in range(ODD)]
        x_cut = sem("x_cut_in_phases")
        x_moved = sem("x_moved_to_phase_rows")
        x_split = sem("x_split")
        conv1_done = sem("conv1_group_done")
        x1_ready = sem("x1_group_evacuated")
        x1_moved = sem("x1_moved_to_channel_rows")
        mix_ready = sem("mixed_matrices_ready")
        m_done = sem("middle_matrix_in_psum")
        m_ready = sem("middle_matrix_in_sbuf")
        v_done = sem("middle_vector_in_psum")
        v_ready = sem("middle_vector_masked")
        b_done = sem("middle_bias_in_psum")
        b_ready = sem("middle_bias_in_sbuf")
        mid_done = sem("middle_group_done")
        x3_hi_ready = sem("x3_high_ready")
        x3_lo_ready = sem("x3_low_ready")
        bias4_ready = sem("bias4_ready")
        conv4_done = sem("conv4_group_done")
        x4_ready = sem("x4_group_evacuated")
        x4_moved = sem("x4_moved_to_channel_rows")
        x_joined = sem("x_out_phases_joined")
        x_stored = [sem(f"x_stored{n}") for n in range(ODD)]

        SETUP_LOADS = [(cond_t, a["cond_t"]), (side, a["side"])]
        for l in range(2):
            SETUP_LOADS += [(w0[l], a[f"w0_{l}"]), (w1[l], a[f"w1_{l}"]), (w2[l], a[f"w2_{l}"]),
                            (b0[l], a[f"b0_{l}"]), (b1[l], a[f"b1_{l}"]), (b2[l], a[f"b2_{l}"]),
                            (cw[l], a[f"cw{l}"]), (bias_k[l], a[f"bias_k{l}"])]
        EXPERT_LOADS = 2
        ALL_ZEROED = 2 + 4 * 2
        THIRDS = 3
        THIRD = B * KI // THIRDS
        ALL_LOADED = DMA * (len(SETUP_LOADS) + EXPERT_LOADS)

        def wait(eng, s, value):
            if not (isinstance(value, int) and value <= 0):
                eng.wait_ge(s, value)

        block = ctx.enter_context(nc.Block())

        @block.sync
        def _(sp):
            def load(b, slot):
                sp.dma_start(x_in[:, slot, :], a["x"][b, :, :]).then_inc(x_loaded[slot], DMA)

            def move_x(b):
                for g in range(G):
                    sp.dma_start(x_ph[:, g, :], x_ch[GROUP * g:GROUP * (g + 1), :, :]
                                 ).then_inc(x_moved, DMA)

            def move_x1(b, g):
                sp.wait_ge(x1_ready, G * b + g + 1)
                sp.dma_start(x1_ch[GROUP * g:GROUP * (g + 1), :, :], x1_ph[:, g, :]
                             ).then_inc(x1_moved, DMA)

            def move_x4(b):
                wait(sp, x_joined, b)
                for g in range(G):
                    sp.wait_ge(x4_ready, G * b + g + 1)
                    sp.dma_start(x4_ch[GROUP * g:GROUP * (g + 1), :, :],
                                 x4_ph[:, g, :]).then_inc(x4_moved, DMA)

            def store(b, slot):
                sp.dma_start(out[b, :, :], x_out[:, slot, :]).then_inc(x_stored[slot], DMA)

            def step(b, slot, whole=True):
                move_x1(b, 0)
                if whole or b + 1 < B:
                    move_x(b + 1)
                if whole or b + 3 < B:
                    load(b + 3, (slot + 3) % ODD)
                for g in range(1, G):
                    move_x1(b, g)
                if whole or b >= 1:
                    move_x4(b - 1)
                if whole or b >= 2:
                    store(b - 2, slot)

            def place_taps(l):
                sp.wait_ge(band_zeroed, l + 1)
                w = a[f"W{l}"].rearrange("c (k g o) -> c k g o", k=TAPS, g=G)
                for p in range(PH):
                    rows = (slice(p, PH * (GROUP - 1) + p + 1, PH), slice(GROUP * p, GROUP * (p + 1)))[l]
                    for q in range(PH):
                        ms = [m for m in range(BLK) if 0 <= PH * m + p - q < TAPS]
                        first = PH * ms[0] + p - q
                        sp.dma_start(band[l][rows, ms[0]:ms[-1] + 1, q, :, :],
                                     w[:, first:first + PH * (len(ms) - 1) + 1:PH, :, :]
                                     ).then_inc(taps_placed[l], DMA)

            load(0, 0)
            load(1, 1)
            place_taps(0)
            sp.wait_ge(x_cut, 1)
            move_x(0)
            load(2, 0)
            place_taps(1)
            for b in range(2):
                step(b, b, whole=False)
            with sp.Fori(1, (B - 4) // 2) as i:
                for odd in range(ODD):
                    step(2 * i + odd, odd)
            for b in range(B - 4, B):
                step(b, b % ODD, whole=False)
            move_x4(B - 1)
            store(B - 2, 0)
            sp.wait_ge(x_joined, B)
            store(B - 1, 1)
            for slot in range(ODD):
                sp.wait_ge(x_stored[slot], DMA * B // ODD)

        @block.gpsimd
        def _(pool):
            pool.memset(ident[:, :], 0.0).then_inc(zeroed, 1)
            pool.memset(ones[:, :], 1.0).then_inc(zeroed, 1)
            for h in (x_hi, x_lo, x3_hi, x3_lo):
                for edge in (h[:, :, 0:HALO], h[:, :, N + HALO:N + 2 * HALO]):
                    pool.memset(edge.bitcast(f32), 0.0).then_inc(zeroed, 1)
            for l in range(2):
                pool.memset(band[l][:, :, :, :, :], 0.0).then_inc(band_zeroed, 1)
            pool.wait_ge(zeroed, ALL_ZEROED)
            pool.affine_select(out=ident[:, :], in_=ident[:, :], compare_op=ALU.not_equal, fill=1.0,
                               base=0, pattern=[[-1, C]], channel_multiplier=1
                               ).then_inc(ident_ready, 1)

        @block.scalar
        def _(act):
            def cut(b, slot, turn):
                act.wait_ge(x_loaded[slot], DMA * (turn + 1))
                wait(act, x_moved, DMA * G * b)
                nc.scalar.copy(x_ch[:, :, :], x_in[:, slot, :].rearrange("c (n p) -> c p n", p=PH)
                               ).then_inc(x_cut, 1)

            for to, of in SETUP_LOADS:
                act.dma_start(to[:, :], of).then_inc(s_in, DMA)
            for l in range(2):
                act.dma_start(expert[l][:, 0:K, :], a[f"e{l}"].rearrange("k r c -> r k c")
                              ).then_inc(s_in, DMA)
            cut(0, 0, 0)
            cut(1, 1, 0)
            act.wait_ge(s_in, ALL_LOADED)
            for l in range(2):
                act.wait_ge(h1_done, l + 1)
                nc.scalar.activation(h1[l][:, :], bank[l][:, 0:B], ACT.Gelu, bias=b0[l][:, :]
                                     ).then_inc(h1_ready, 1)
            for l in range(2):
                act.wait_ge(h2_done, l + 1)
                nc.scalar.activation(h2[l][:, :], bank[2 + l][:, 0:B], ACT.Gelu, bias=b1[l][:, :]
                                     ).then_inc(h2_ready, 1)
            for l in range(2):
                act.wait_ge(top_ready, l + 1)
                nc.scalar.activation(att[l][:, 0:K], bank[4 + l][0:B, 0:K], ACT.Exp, bias=top[l][:, :],
                                     accum_out=total[l][:, :]).then_inc(exp_ready, 1)

            def join(b, slot, turn):
                act.wait_ge(x4_moved, DMA * G * (b + 1))
                wait(act, x_stored[slot], DMA * turn)
                nc.scalar.copy(x_out[:, slot, :].rearrange("c (n p) -> c p n", p=PH), x4_ch[:, :, :]
                               ).then_inc(x_joined, 1)

            def evacuate_x1(b):
                wait(act, x1_moved, DMA * G * b)
                for g in range(G):
                    act.wait_ge(conv1_done, G * b + g + 1)
                    nc.scalar.copy(x1_ph[:, g, :], conv_bank[g % 2][:, :]).then_inc(x1_ready, 1)

            def evacuate_x4(b):
                act.wait_ge(bias4_ready, b + 1)
                wait(act, x4_moved, DMA * G * b)
                for g in range(G):
                    act.wait_ge(conv4_done, G * b + g + 1)
                    nc.scalar.activation(x4_ph[:, g, :], conv_bank[g % 2][:, :], ACT.Identity,
                                         bias=bias4_now[:, g:g + 1]).then_inc(x4_ready, 1)

            def round_x3(b):
                act.wait_ge(b_ready, b + 1)
                for g in range(G):
                    act.wait_ge(mid_done, G * b + g + 1)
                    nc.scalar.activation(x3_hi[:, g, HALO:N + HALO], mid_bank[g][:, :], ACT.Identity,
                                         bias=bias3_now[:, g:g + 1]).then_inc(x3_hi_ready, 1)

            def step(b, slot, turn, first=False, last=False):
                evacuate_x1(b)
                if not last:
                    cut(b + 2, slot, turn + 1)
                if not first:
                    evacuate_x4(b - 1)
                round_x3(b)
                if not first:
                    join(b - 1, 1 - slot, turn - 1 + slot)

            for b in range(2 * ODD):
                step(b, b % ODD, b // ODD, first=(b == 0))
            with act.Fori(2, B // ODD - 1) as i:
                for odd in range(ODD):
                    step(ODD * i + odd, odd, i)
            for b in range(B - ODD, B):
                step(b, b % ODD, b // ODD, last=True)
            evacuate_x4(B - 1)
            join(B - 1, (B - 1) % ODD, (B - 1) // ODD)

        @block.vector
        def _(dve):
            dve.wait_ge(ident_ready, 1)
            nc.vector.tensor_reduce(in_rank[:, :], ident[:, :].rearrange("p (g c) -> p c g", g=G),
                                    AX.X, ALU.add).then_inc(masks_ready, 1)
            nc.vector.tensor_reduce(in_group[:, :], ident[:, :].rearrange("p (g c) -> p g c", g=G),
                                    AX.X, ALU.add).then_inc(masks_ready, 1)
            dve.wait_ge(masks_ready, 2)
            nc.vector.tensor_copy(spread_qc[:, :, :],
                                  in_rank[:, :].unsqueeze(1).broadcast_to([C, PH, GROUP])
                                  ).then_inc(masks_ready, 1)
            nc.vector.tensor_copy(spread_cq[:, :, :],
                                  in_rank[:, :].unsqueeze(2).broadcast_to([C, GROUP, PH])
                                  ).then_inc(masks_ready, 1)
            for l in range(2):
                nc.vector.tensor_copy(expert[l][:, K, :], ident[:, :]).then_inc(eye_ready, 1)
                nc.vector.memset(att[l][:, K:KI], 1.0).then_inc(eye_ready, 1)
            dve.wait_ge(s_in, ALL_LOADED)
            for l, to in enumerate((bias1, bias4_ch)):
                dve.wait_ge(ctx_done, l + 1)
                nc.vector.tensor_scalar(to[:, :], bank[6 + l][:, 0:B], side[:, :], None, ALU.add
                                        ).then_inc(ctx_ready, 1)
            dve.wait_ge(ctx_ready, 2)
            nc.vector.tensor_tensor(bias4_g, bias4_ch[:, :].unsqueeze(1).broadcast_to([C, G, B]),
                                    in_group[:, :].unsqueeze(2).broadcast_to([C, G, B]), ALU.mult
                                    ).then_inc(bias4_g_ready, 1)

            def split_x(b):
                dve.wait_ge(x_moved, DMA * G * (b + 1))
                wait(dve, conv1_done, G * b)
                nc.vector.tensor_copy(x_hi[:, :, HALO:N + HALO], x_ph[:, :, :]).then_inc(x_split, 1)
                dve.wait_ge(x_split, 2 * b + 1)
                nc.vector.tensor_tensor(x_lo[:, :, HALO:N + HALO], x_ph[:, :, :],
                                        x_hi[:, :, HALO:N + HALO].bitcast(f32), ALU.subtract
                                        ).then_inc(x_split, 1)

            def conv_weights(l):
                dve.wait_ge(taps_placed[l], DMA * PH * PH)
                middle = band[l][:, HALO, :, :, :]
                if l == 0:
                    middle = middle.rearrange("r q g o -> r g o q")
                    same = ident[:, :].rearrange("r (o q) -> r o q", q=PH)
                else:
                    middle = middle.rearrange("r q g o -> r g q o")
                    same = ident[:, :].rearrange("r (q o) -> r q o", q=PH)
                nc.vector.tensor_tensor(middle, middle,
                                        same.unsqueeze(1).broadcast_to([C, G, *same.shape[1:]]),
                                        ALU.add).then_inc(band_ready, 1)
                dve.wait_ge(band_ready, l + 1)
                for m in range(BLK):
                    whole = band[l][:, m, :, :, :].rearrange("r q g o -> r g o q")
                    hi, lo = (w[l][:, m, :, :].rearrange("r g (o q) -> r g o q", q=PH)
                              for w in (w_hi, w_lo))
                    nc.vector.tensor_copy(hi, whole).then_inc(w_hi_ready, 1)
                    dve.wait_ge(w_hi_ready, BLK * l + m + 1)
                    nc.vector.tensor_tensor(lo, whole, hi.bitcast(f32), ALU.subtract
                                            ).then_inc(w_lo_ready, 1)

            conv_weights(0)
            split_x(0)

            for l in range(2):
                dve.wait_ge(score_done, l + 1)
                nc.vector.tensor_reduce(top[l][:, :], bank[4 + l][0:B, 0:K], AX.X, ALU.max, negate=True
                                        ).then_inc(top_ready, 1)
            for l in range(2):
                dve.wait_ge(exp_ready, l + 1)
                nc.vector.reciprocal(share[l][:, :], total[l][:, :]).then_inc(share_ready, 1)
                dve.wait_ge(share_ready, l + 1)
                nc.vector.tensor_scalar(att[l][:, 0:K], att[l][:, 0:K], share[l][:, :], None, ALU.mult
                                        ).then_inc(att_ready, 1)
                dve.wait_ge(att_ready, l + 1)
                dve.wait_ge(eye_ready, 4)
                nc.vector.tensor_tensor(att_diag[l].rearrange("p (b k) -> p b k", k=KI),
                                        att[l][:, :].unsqueeze(1).broadcast_to([B, B, KI]),
                                        ident[0:B, 0:B].unsqueeze(2).broadcast_to([B, B, KI]), ALU.mult
                                        ).then_inc(diag_ready, 1)
            for l in range(2):
                dve.wait_ge(att_t_done, l + 1)
                nc.vector.tensor_copy(att_t[l][:, :], bank[l][0:K, 0:B]).then_inc(att_t_ready, 1)
            for l in range(2):
                for n in range(THIRDS):
                    dve.wait_ge(mix_done, THIRDS * l + n + 1)
                    nc.vector.tensor_copy(
                        mix[l][:, :, :].rearrange("p b k -> p (b k)")[:, n * THIRD:(n + 1) * THIRD],
                        bank[2 + n][:, 0:THIRD]).then_inc(mix_copied, 1)
            for l in range(2):
                dve.wait_ge(bias_l_done, l + 1)
                nc.vector.tensor_copy(bias_l[l][:, :], bank[l][:, 0:B]).then_inc(bias_l_ready, 1)
            dve.wait_ge(bias4_done, 1)
            nc.vector.tensor_copy(bias4[:, :, :].rearrange("p g b -> p (g b)"), bank[7][:, 0:G * B]
                                  ).then_inc(bias4_all, 1)
            dve.wait_ge(mix_copied, 2 * THIRDS)
            dve.wait_ge(bias4_all, 1)
            dve.wait_ge(bias_l_ready, 2)

            def mix_experts(b, l):
                wait(dve, mix_ready, 2 * b + l)
                nc.vector.tensor_tensor(weighted[:, :, :], expert[l][:, :, :],
                                        mix[l][:, b, :].unsqueeze(2).broadcast_to([C, KI, C]),
                                        ALU.mult).then_inc(weighted_ready, 1)
                dve.wait_ge(weighted_ready, 2 * b + l + 1)
                nc.vector.tensor_reduce(mixed[l][:, :], weighted[:, :, :].rearrange("p k c -> p c k"),
                                        AX.X, ALU.add).then_inc(mix_ready, 1)

            def copy_m(b):
                dve.wait_ge(m_done, b + 1)
                nc.vector.tensor_copy(m_t[:, :], m_ps).then_inc(m_ready, 1)

            def mask_vector(b):
                dve.wait_ge(v_done, b + 1)
                nc.vector.scalar_tensor_tensor(vec_g[:, :], v_ps.broadcast_to([C, G]),
                                               bias_l[1][:, bass.ds(b, 1)], in_group[:, :],
                                               op0=ALU.add, op1=ALU.mult).then_inc(v_ready, 1)

            def copy_bias3(b):
                dve.wait_ge(b_done, b + 1)
                nc.vector.tensor_copy(bias3_now[:, :], b_ps).then_inc(b_ready, 1)

            def set_bias4(b):
                wait(dve, x4_ready, G * b)
                nc.vector.tensor_scalar(bias4_now[:, :], bias4[:, :, b], 0.0, None, ALU.add
                                        ).then_inc(bias4_ready, 1)

            def low_x3(b):
                for g in range(G):
                    dve.wait_ge(x3_hi_ready, G * b + g + 1)
                    nc.vector.scalar_tensor_tensor(x3_lo[:, g, HALO:N + HALO], mid_bank[g][:, :],
                                                   bias3_now[:, g:g + 1],
                                                   x3_hi[:, g, HALO:N + HALO].bitcast(f32),
                                                   op0=ALU.add, op1=ALU.subtract
                                                   ).then_inc(x3_lo_ready, 1)

            def step(b, last=False):
                copy_m(b)
                if not last:
                    mix_experts(b + 1, 0)
                mask_vector(b)
                if not last:
                    mix_experts(b + 1, 1)
                copy_bias3(b)
                if not last:
                    split_x(b + 1)
                set_bias4(b)
                low_x3(b)

            for l in range(2):
                mix_experts(0, l)
            conv_weights(1)
            step(0)
            with dve.Fori(1, B - 1) as b:
                step(b)
            step(B - 1, last=True)

        @block.tensor
        def _(pe):
            pe.wait_ge(s_in, ALL_LOADED)
            for l in range(2):
                nc.tensor.matmul(bank[l][:, 0:B], w0[l][:, :], cond_t[:, :], start=True, stop=True
                                 ).then_inc(h1_done, 1)
            for l in range(2):
                nc.tensor.matmul(bank[6 + l][:, 0:B], cw[l][:, :], cond_t[:, :], start=True, stop=True
                                 ).then_inc(ctx_done, 1)
            for l in range(2):
                pe.wait_ge(h1_ready, l + 1)
                nc.tensor.matmul(bank[2 + l][:, 0:B], w1[l][:, :], h1[l][:, :], start=True, stop=True
                                 ).then_inc(h2_done, 1)
            pe.wait_ge(ident_ready, 1)
            for l in range(2):
                pe.wait_ge(h2_ready, l + 1)
                nc.tensor.matmul(bank[4 + l][0:B, 0:K], h2[l][:, :], w2[l][:, :], start=True, stop=False)
                nc.tensor.matmul(bank[4 + l][0:B, 0:K], ones[0:1, 0:B], b2[l][:, :], start=False,
                                 stop=True).then_inc(score_done, 1)
            pe.wait_ge(bias4_g_ready, 1)
            pe.wait_ge(masks_ready, 4)
            nc.tensor.matmul(bank[7][:, 0:G * B], spread_cq[:, :, :].rearrange("p c q -> p (c q)"),
                             bias4_g.rearrange("p g b -> p (g b)"), start=True, stop=True
                             ).then_inc(bias4_done, 1)
            for l in range(2):
                pe.wait_ge(h1_ready, l + 1)
                pe.wait_ge(att_ready, l + 1)
                nc.tensor.transpose(bank[l][0:K, 0:B], att[l][:, 0:K], ident[0:B, 0:B]
                                    ).then_inc(att_t_done, 1)
            for l in range(2):
                pe.wait_ge(diag_ready, l + 1)
                for n in range(THIRDS):
                    if l == 0:
                        pe.wait_ge(exp_ready, 2)
                    else:
                        pe.wait_ge(mix_copied, n + 1)
                    nc.tensor.matmul(bank[2 + n][:, 0:THIRD], ones[0:B, :],
                                     att_diag[l][:, n * THIRD:(n + 1) * THIRD], start=True, stop=True
                                     ).then_inc(mix_done, 1)
            for l in range(2):
                pe.wait_ge(att_t_ready, l + 1)
                nc.tensor.matmul(bank[l][:, 0:B], bias_k[l][:, :], att_t[l][:, :], start=True,
                                 stop=True).then_inc(bias_l_done, 1)
            pe.wait_ge(mix_copied, 2 * THIRDS)
            pe.wait_ge(bias_l_ready, 2)

            def conv(l, g, hi, lo, done):
                parts = ((w_hi, hi), (w_hi, lo), (w_lo, hi))
                last = len(parts) * BLK - 1
                for n in range(last + 1):
                    w, x = parts[n // BLK]
                    m = n % BLK
                    mm = nc.tensor.matmul(conv_bank[g % 2][:, :], w[l][:, m, g, :], x[:, g, m:m + N],
                                          start=(n == 0), stop=(n == last))
                mm.then_inc(done, 1)

            def conv1(b):
                pe.wait_ge(x_split, 2 * b + 2)
                for g in range(G):
                    if g >= 2:
                        pe.wait_ge(x1_ready, G * b + g - 1)
                    elif isinstance(b, int) and b == 1:
                        pe.wait_ge(x1_ready, g + 3)
                    elif not isinstance(b, int) or b >= 2:
                        pe.wait_ge(x4_ready, G * (b - 2) + g + 3)
                    conv(0, g, x_hi, x_lo, conv1_done)
                    if g == 1:
                        middle_vector(b)
                middle_bias(b)

            def conv4(b, after_x4=False):
                for g in range(G):
                    pe.wait_ge(x3_lo_ready, G * b + g + 1)
                    if g >= 2:
                        pe.wait_ge(x4_ready, G * b + g - 1)
                    elif after_x4:
                        pe.wait_ge(x4_ready, G * (b - 1) + g + 3)
                    else:
                        pe.wait_ge(x1_ready, G * (b + 1) + g + 3)
                    conv(1, g, x3_hi, x3_lo, conv4_done)

            def middle_matrix(b):
                pe.wait_ge(mix_ready, 2 * b + 2)
                wait(pe, b_ready, b)
                nc.tensor.matmul(m_ps, mixed[0][:, :], mixed[1][:, :], start=True, stop=True
                                 ).then_inc(m_done, 1)

            def middle_vector(b):
                pe.wait_ge(m_ready, b + 1)
                nc.tensor.matmul(v_ps, m_t[:, :], bias1[:, bass.ds(b, 1)], start=True, stop=False)
                nc.tensor.matmul(v_ps, mixed[1][:, :], bias_l[0][:, bass.ds(b, 1)], start=False, stop=True
                                 ).then_inc(v_done, 1)

            def middle_bias(b):
                pe.wait_ge(v_ready, b + 1)
                nc.tensor.matmul(b_ps, spread_qc[:, :, :].rearrange("p q c -> p (q c)"), vec_g[:, :],
                                 start=True, stop=True).then_inc(b_done, 1)

            def middle(b):
                pe.wait_ge(x1_moved, DMA * G * (b + 1))
                for g in range(G):
                    wait(pe, x3_lo_ready, G * (b - 1) + g + 1)
                    for q in range(PH):
                        mm = nc.tensor.matmul(mid_bank[g][GROUP * q:GROUP * (q + 1), :],
                                              m_t[:, GROUP * g:GROUP * (g + 1)], x1_ch[:, q, :],
                                              start=True, stop=True)
                    mm.then_inc(mid_done, 1)

            def step(b):
                middle_matrix(b)
                conv1(b)
                if not isinstance(b, int) or b >= 1:
                    conv4(b - 1)
                middle(b)

            pe.wait_ge(w_lo_ready, BLK)
            step(0)
            pe.wait_ge(w_lo_ready, 2 * BLK)
            step(1)
            with pe.Fori(2, B) as b:
                step(b)
            conv4(B - 1, after_x4=True)


def kernel(**inputs):
    import numpy as np
    import concourse.bacc as bacc
    from concourse.bass_utils import run_bass_kernel_spmd

    def grouped(w):
        out_c, in_c, k = w.shape
        return w.reshape(out_c // in_c, in_c, in_c, k).transpose(2, 3, 0, 1).reshape(in_c, -1)

    v = {n: np.asarray(x) for n, x in inputs.items()}
    laid = {
        "x": v["x"], "cond_t": v["cond_128"].T, "side": v["fside_S_0"][:, None],
        "W0": grouped(v["L0_cond_weight"]), "W1": grouped(v["L3_cond_weight"]),
        "cw0": v["L0_cond_c_weight"].T, "cw1": v["L3_cond_c_weight"].T,
        "e0": v["L1_cond_weight"][..., 0], "e1": v["L2_cond_weight"][..., 0].transpose(0, 2, 1),
    }
    for l in range(2):
        n = f"L{l + 1}_cond_"
        laid |= {f"w0_{l}": v[n + "W0"], f"w1_{l}": v[n + "W1"], f"w2_{l}": v[n + "W2"],
                 f"b0_{l}": v[n + "b0"][:, None], f"b1_{l}": v[n + "b1"][:, None],
                 f"b2_{l}": v[n + "b2"][None, :], f"bias_k{l}": v[n + "bias_k"]}
    nc = bacc.Bacc("TRN2", target_bir_lowering=False, num_devices=1)
    arrays, args = {}, {}
    for name, x in laid.items():
        x = np.ascontiguousarray(x)
        arrays[f"in_{name}"] = x
        args[name] = nc.dram_tensor(f"in_{name}", x.shape, mybir.dt.from_np(x.dtype),
                                    kind="ExternalInput").ap()
    out = nc.dram_tensor("out", v["x"].shape, mybir.dt.from_np(v["x"].dtype),
                         kind="ExternalOutput").ap()
    cond_resid_kernel(nc, args, out)
    return run_bass_kernel_spmd(nc, [arrays], core_ids=[0]).results[0]["out"]
```

```python
import concourse.bass as bass
from concourse import mybir
from contextlib import ExitStack


def cond_resid_kernel(nc: bass.Bass, a, out):
    f32, f32r = mybir.dt.float32, mybir.dt.float32r
    ALU, ACT, AX = mybir.AluOpType, mybir.ActivationFunctionType, mybir.AxisListType

    B, C, L = a["x"].shape
    GROUP = a["W0"].shape[0]
    TAPS = a["W0"].shape[1] // C
    G = C // GROUP
    PH = C // GROUP
    N = L // PH
    BLK = (PH + TAPS - 1) // PH
    HALO = BLK // 2
    K = a["e0"].shape[0]
    KI = K + 1
    DMA = 16
    ODD = 2

    ctx = ExitStack()
    with ctx:
        def sb(name, shape, dt=f32):
            return ctx.enter_context(nc.sbuf_tensor(name, shape, dt))

        def sem(name):
            return ctx.enter_context(nc.semaphore(name))

        x_in = sb("x_in", [C, ODD, L])
        x_ch = sb("x_ch", [C, PH, N])
        x_ph = sb("x_ph", [C, G, N])
        x_hi = sb("x_hi", [C, G, N + 2 * HALO], f32r)
        x_lo = sb("x_lo", [C, G, N + 2 * HALO], f32r)
        x1_ph = sb("x1_ph", [C, G, N])
        x1_ch = sb("x1_ch", [C, PH, N])
        x1_hi = sb("x1_hi", [C, PH, N], f32r)
        x1_lo = sb("x1_lo", [C, PH, N], f32r)
        x3_ch = sb("x3_ch", [C, PH, N])
        x3_ph = sb("x3_ph", [C, G, N])
        x3_hi = sb("x3_hi", [C, G, N + 2 * HALO], f32r)
        x3_lo = sb("x3_lo", [C, G, N + 2 * HALO], f32r)
        x4_ph = sb("x4_ph", [C, G, N])
        x4_ch = sb("x4_ch", [C, PH, N])
        x_out = sb("x_out", [C, ODD, L])
        band = [x_out[:, l, 0:BLK * PH * C].rearrange("r (m q g o) -> r m q g o", m=BLK, q=PH, g=G)
                for l in range(2)]
        w_hi = [sb(f"w_hi{l}", [C, BLK, G, C], f32r) for l in range(2)]
        w_lo = [sb(f"w_lo{l}", [C, BLK, G, C], f32r) for l in range(2)]
        expert = [sb(f"expert{l}", [C, KI, C]) for l in range(2)]
        mix = [sb(f"mix{l}", [C, B, KI]) for l in range(2)]
        weighted = sb("weighted", [C, KI, C])
        mixed = [sb(f"mixed{l}", [C, C]) for l in range(2)]
        m_t = sb("m_t", [C, C])
        m_hi = sb("m_hi", [C, C], f32r)
        m_lo = sb("m_lo", [C, C], f32r)
        bias1 = sb("bias1", [C, B])
        bias_l = [sb(f"bias_l{l}", [C, B]) for l in range(2)]
        bias4_ch = sb("bias4_ch", [C, B])
        bias4 = sb("bias4", [C, G, B])
        bias3 = sb("bias3", [C, B])
        carried = sb("carried", [C, B])
        bias3_now = sb("bias3_now", [C, 1])
        bias4_now = sb("bias4_now", [C, G])
        ident = sb("ident", [C, C])
        ones = sb("ones", [C, C])
        in_rank = sb("in_rank", [C, GROUP])
        spread_cq = sb("spread_cq", [C, GROUP, PH])
        in_group = sb("in_group", [C, G])
        side = sb("side", [C, 1])
        w2 = [sb(f"w2_{l}", [C, K]) for l in range(2)]
        b0 = [sb(f"b0_{l}", [C, 1]) for l in range(2)]
        b1 = [sb(f"b1_{l}", [C, 1]) for l in range(2)]
        b2 = [sb(f"b2_{l}", [1, K]) for l in range(2)]
        bias_k = [sb(f"bias_k{l}", [K, C]) for l in range(2)]
        top = [sb(f"top{l}", [B, 1]) for l in range(2)]
        total = [sb(f"total{l}", [B, 1]) for l in range(2)]
        share = [sb(f"share{l}", [B, 1]) for l in range(2)]
        att = [sb(f"att{l}", [B, KI]) for l in range(2)]
        att_t = [sb(f"att_t{l}", [K, B]) for l in range(2)]
        att_diag = [t.rearrange("p g n -> p (g n)")[:, 0:B * KI] for t in (x1_ch[0:B, :, :], x4_ch[0:B, :, :])]
        expert_t = x3_ph[:, :, :].rearrange("p g n -> p (g n)")[:, 0:K * C].rearrange(
            "p (k c) -> p k c", k=K)
        vec_part = x3_ch[:, :, :].rearrange("p q n -> p (q n)")[:, 0:B * K].rearrange(
            "p (b k) -> p b k", k=K)
        spare = x3_ph[:, G // 2:, :].rearrange("p g n -> p (g n)")
        w0, w1, cw = ([spare[:, (2 * n + l) * C:(2 * n + l + 1) * C] for l in range(2)] for n in range(3))
        cond_t = spare[:, 6 * C:6 * C + B]
        spare = x3_ch[:, PH // 2:, :].rearrange("p q n -> p (q n)")
        h1, h2 = ([spare[:, (2 * n + l) * B:(2 * n + l + 1) * B] for l in range(2)] for n in range(2))
        bias4_g = x4_ph[:, 0, 0:G * B].rearrange("p (g b) -> p g b", g=G)

        pair = [ctx.enter_context(nc.psum_tensor(f"pair{n}", [C, 2, N], f32)) for n in range(2)]
        quad = ctx.enter_context(nc.psum_tensor("quad", [C, PH, N], f32))
        bank = [pair[0][:, 0, :], pair[0][:, 1, :], *(quad[:, n, :] for n in range(PH)),
                pair[1][:, 0, :], pair[1][:, 1, :]]
        conv_bank = bank[0:2]
        mid_bank = quad
        m_ps = bank[6][:, 0:C]
        vec_ps = pair[1][:, :, 0:K // 2 * B]

        s_in = sem("setup_loaded")
        taps_placed = [sem(f"conv_taps_placed{l}") for l in range(2)]
        zeroed = sem("ident_ones_halos_filled")
        ident_ready = sem("identity_ready")
        h1_done = sem("hidden1_in_psum")
        h1_ready = sem("hidden1_in_sbuf")
        h2_done = sem("hidden2_in_psum")
        h2_ready = sem("hidden2_in_sbuf")
        score_done = sem("scores_in_psum")
        top_ready = sem("score_maximum_negated")
        exp_ready = sem("exponentials_ready")
        share_ready = sem("one_over_their_sum")
        att_ready = sem("attention_ready")
        diag_ready = sem("attention_on_diagonal")
        att_t_done = sem("attention_transposed_in_psum")
        att_t_ready = sem("attention_transposed_in_sbuf")
        mix_done = sem("mix_third_in_psum")
        mix_copied = sem("mix_third_in_sbuf")
        bias_l_done = sem("layer_bias_in_psum")
        bias_l_ready = sem("layer_bias_in_sbuf")
        ctx_done = sem("context_in_psum")
        ctx_ready = sem("context_bias_in_sbuf")
        masks_ready = sem("spread_and_group_masks")
        bias4_g_ready = sem("bias4_masked_by_group")
        bias4_done = sem("bias4_in_psum")
        bias4_all = sem("bias4_in_sbuf")
        vec_done = sem("expert_vectors_in_psum")
        vec_weighted = sem("expert_vectors_weighted")
        vec_summed = sem("expert_vectors_summed")
        vec_ready = sem("vector_after_layer_ready")
        eye_ready = sem("identity_expert_written")
        band_zeroed = sem("band_zeroed")
        band_ready = sem("band_with_residual")
        w_hi_ready = sem("conv_weights_high")
        w_lo_ready = sem("conv_weights_low")
        weighted_ready = sem("experts_weighted")
        x_loaded = [sem(f"x_loaded{n}") for n in range(ODD)]
        x_cut = sem("x_half_cut_in_phases")
        x_moved = sem("x_moved_to_phase_rows")
        x_hi_ready = sem("x_high_ready")
        x_lo_ready = sem("x_low_ready")
        conv1_done = sem("conv1_group_done")
        x1_ready = sem("x1_group_evacuated")
        x1_moved = sem("x1_moved_to_channel_rows")
        mix_ready = sem("mixed_matrices_ready")
        m_done = sem("middle_matrix_in_psum")
        m_ready = sem("middle_matrix_in_sbuf")
        m_split = sem("middle_matrix_split")
        bias3_ready = sem("x3_bias_ready")
        x1_high = sem("x1_phase_high_ready")
        x1_split = sem("x1_phase_split")
        mid_done = sem("middle_phase_done")
        x3_ready = sem("x3_half_evacuated")
        x3_moved = [sem(f"x3_group{g}_moved_to_phase_rows") for g in range(G)]
        x3_high = sem("x3_group_high_ready")
        x3_split = sem("x3_group_split")
        bias4_ready = sem("bias4_ready")
        conv4_done = sem("conv4_group_done")
        x4_ready = sem("x4_group_evacuated")
        x4_moved = sem("x4_moved_to_channel_rows")
        x_joined = sem("x_out_half_joined")
        x_stored = [sem(f"x_stored{n}") for n in range(ODD)]

        SETUP_LOADS = [(cond_t, a["cond_t"]), (side, a["side"])]
        for l in range(2):
            SETUP_LOADS += [(w0[l], a[f"w0_{l}"]), (w1[l], a[f"w1_{l}"]), (w2[l], a[f"w2_{l}"]),
                            (b0[l], a[f"b0_{l}"]), (b1[l], a[f"b1_{l}"]), (b2[l], a[f"b2_{l}"]),
                            (cw[l], a[f"cw{l}"]), (bias_k[l], a[f"bias_k{l}"])]
        EXPERT_LOADS = 3
        ALL_ZEROED = 2 + 4 * 2
        THIRDS = 3
        THIRD = B * KI // THIRDS
        ALL_LOADED = DMA * (len(SETUP_LOADS) + EXPERT_LOADS)

        def wait(eng, s, value):
            if not (isinstance(value, int) and value <= 0):
                eng.wait_ge(s, value)

        block = ctx.enter_context(nc.Block())

        @block.sync
        def _(sp):
            def load(b, slot):
                sp.dma_start(x_in[:, slot, :], a["x"][b, :, :]).then_inc(x_loaded[slot], DMA)

            def move_x(b):
                for g in range(G):
                    sp.dma_start(x_ph[:, g, :], x_ch[GROUP * g:GROUP * (g + 1), :, :]
                                 ).then_inc(x_moved, DMA)

            def move_x1(b, g):
                sp.wait_ge(x1_ready, G * b + g + 1)
                sp.dma_start(x1_ch[GROUP * g:GROUP * (g + 1), :, :], x1_ph[:, g, :]
                             ).then_inc(x1_moved, DMA)

            def move_x4(b, g):
                if g == 0:
                    wait(sp, x_joined, 2 * b)
                sp.wait_ge(x4_ready, G * b + g + 1)
                sp.dma_start(x4_ch[GROUP * g:GROUP * (g + 1), :, :], x4_ph[:, g, :]
                             ).then_inc(x4_moved, DMA)

            def store(b, slot):
                sp.dma_start(out[b, :, :], x_out[:, slot, :]).then_inc(x_stored[slot], DMA)

            def move_x3(b):
                sp.wait_ge(x3_ready, 2 * b + 2)
                for g in range(G):
                    sp.dma_start(x3_ph[:, g, :], x3_ch[GROUP * g:GROUP * (g + 1), :, :]
                                 ).then_inc(x3_moved[g], DMA)

            def step(b, slot, whole=True):
                if whole or b >= 1:
                    move_x3(b - 1)
                move_x1(b, 0)
                if whole or b + 1 < B:
                    move_x(b + 1)
                for g in range(1, G):
                    move_x1(b, g)
                if whole or b + 3 < B:
                    load(b + 3, (slot + 3) % ODD)
                for g in range(G):
                    if g == G - 1 and (whole or b >= 2):
                        store(b - 2, slot)
                    if whole or b >= 1:
                        move_x4(b - 1, g)

            def place_taps(l):
                sp.wait_ge(band_zeroed, l + 1)
                w = a[f"W{l}"].rearrange("c (k g o) -> c k g o", k=TAPS, g=G)
                for p in range(PH):
                    rows = slice(p, PH * (GROUP - 1) + p + 1, PH)
                    for q in range(PH):
                        ms = [m for m in range(BLK) if 0 <= PH * m + p - q < TAPS]
                        first = PH * ms[0] + p - q
                        sp.dma_start(band[l][rows, ms[0]:ms[-1] + 1, q, :, :],
                                     w[:, first:first + PH * (len(ms) - 1) + 1:PH, :, :]
                                     ).then_inc(taps_placed[l], DMA)

            load(0, 0)
            load(1, 1)
            place_taps(0)
            sp.wait_ge(x_cut, 2)
            move_x(0)
            load(2, 0)
            place_taps(1)
            for b in range(2):
                step(b, b, whole=False)
            with sp.Fori(1, (B - 4) // 2) as i:
                for odd in range(ODD):
                    step(2 * i + odd, odd)
            for b in range(B - 4, B):
                step(b, b % ODD, whole=False)
            move_x3(B - 1)
            move_x4(B - 1, 0)
            store(B - 2, 0)
            for g in range(1, G):
                move_x4(B - 1, g)
            sp.wait_ge(x_joined, 2 * B)
            store(B - 1, 1)
            for slot in range(ODD):
                sp.wait_ge(x_stored[slot], DMA * B // ODD)

        @block.gpsimd
        def _(pool):
            pool.memset(ident[:, :], 0.0).then_inc(zeroed, 1)
            pool.memset(ones[:, :], 1.0).then_inc(zeroed, 1)
            for h in (x_hi, x_lo, x3_hi, x3_lo):
                for edge in (h[:, :, 0:HALO], h[:, :, N + HALO:N + 2 * HALO]):
                    pool.memset(edge.bitcast(f32), 0.0).then_inc(zeroed, 1)
            for l in range(2):
                pool.memset(band[l][:, :, :, :, :], 0.0).then_inc(band_zeroed, 1)
            pool.wait_ge(zeroed, ALL_ZEROED)
            pool.affine_select(out=ident[:, :], in_=ident[:, :], compare_op=ALU.not_equal, fill=1.0,
                               base=0, pattern=[[-1, C]], channel_multiplier=1
                               ).then_inc(ident_ready, 1)

        @block.scalar
        def _(act):
            def cut(b, slot, turn, half):
                if half == 0:
                    act.wait_ge(x_loaded[slot], DMA * (turn + 1))
                    wait(act, x_moved, DMA * G * b)
                phases = slice(half * PH // 2, (half + 1) * PH // 2)
                nc.scalar.copy(x_ch[:, phases, :],
                               x_in[:, slot, :].rearrange("c (n p) -> c p n", p=PH)[:, phases, :]
                               ).then_inc(x_cut, 1)

            def round_x(b):
                act.wait_ge(x_moved, DMA * G * (b + 1))
                wait(act, conv1_done, G * b)
                nc.scalar.copy(x_hi[:, :, HALO:N + HALO], x_ph[:, :, :]).then_inc(x_hi_ready, 1)

            for to, of in SETUP_LOADS:
                act.dma_start(to[:, :], of).then_inc(s_in, DMA)
            for l in range(2):
                act.dma_start(expert[l][:, 0:K, :], a[f"e{l}"].rearrange("k r c -> r k c")
                              ).then_inc(s_in, DMA)
            act.dma_start(expert_t, a["e0_t"].rearrange("k r c -> r k c")).then_inc(s_in, DMA)
            for half in range(2):
                cut(0, 0, 0, half)
            act.wait_ge(s_in, ALL_LOADED)
            for l in range(2):
                act.wait_ge(h1_done, l + 1)
                nc.scalar.activation(h1[l][:, :], bank[l][:, 0:B], ACT.Gelu, bias=b0[l][:, :]
                                     ).then_inc(h1_ready, 1)
            for l in range(2):
                act.wait_ge(h2_done, l + 1)
                nc.scalar.activation(h2[l][:, :], bank[2 + l][:, 0:B], ACT.Gelu, bias=b1[l][:, :]
                                     ).then_inc(h2_ready, 1)
            round_x(0)
            for l in range(2):
                act.wait_ge(top_ready, l + 1)
                nc.scalar.activation(att[l][:, 0:K], bank[4 + l][0:B, 0:K], ACT.Exp, bias=top[l][:, :],
                                     accum_out=total[l][:, :]).then_inc(exp_ready, 1)

            def join(b, slot, turn, half):
                if half == 0:
                    act.wait_ge(x4_moved, DMA * G * (b + 1))
                    wait(act, x_stored[slot], DMA * turn)
                phases = slice(half * PH // 2, (half + 1) * PH // 2)
                nc.scalar.copy(x_out[:, slot, :].rearrange("c (n p) -> c p n", p=PH)[:, phases, :],
                               x4_ch[:, phases, :]).then_inc(x_joined, 1)

            def evacuate_x1(b, g):
                if g == 0:
                    wait(act, x1_moved, DMA * G * b)
                act.wait_ge(conv1_done, G * b + g + 1)
                nc.scalar.copy(x1_ph[:, g, :], conv_bank[g % 2]).then_inc(x1_ready, 1)

            def evacuate_x4(b, g):
                if g == 0:
                    act.wait_ge(bias4_ready, b + 1)
                    wait(act, x4_moved, DMA * G * b)
                act.wait_ge(conv4_done, G * b + g + 1)
                nc.scalar.activation(x4_ph[:, g, :], conv_bank[g % 2], ACT.Identity,
                                     bias=bias4_now[:, g:g + 1]).then_inc(x4_ready, 1)

            def evacuate_x3(b):
                act.wait_ge(bias3_ready, b + 1)
                for half in range(2):
                    act.wait_ge(mid_done, PH * b + PH // 2 * (half + 1))
                    phases = slice(half * PH // 2, (half + 1) * PH // 2)
                    nc.scalar.activation(x3_ch[:, phases, :], mid_bank[:, phases, :], ACT.Identity,
                                         bias=bias3_now[:, :]).then_inc(x3_ready, 1)

            def step(b, slot, turn, first=False, last=False):
                evacuate_x1(b, 0)
                if not first:
                    join(b - 2, slot, turn - 1, 0)
                evacuate_x1(b, 1)
                if not first:
                    join(b - 2, slot, turn - 1, 1)
                evacuate_x1(b, 2)
                evacuate_x1(b, 3)
                for g in range(G):
                    if not (isinstance(b, int) and b == 0):
                        evacuate_x4(b - 1, g)
                    if g == 0 and not (last and slot == 1):
                        round_x(b + 1)
                    if not last and g in (1, 2):
                        cut(b + 2, slot, turn + 1, g - 1)
                evacuate_x3(b)

            for half in range(2):
                cut(1, 1, 0, half)
            for b in range(2 * ODD):
                step(b, b % ODD, b // ODD, first=(b < 2))
                if b == 1:
                    act.wait_ge(w_lo_ready, 2 * BLK)
            with act.Fori(2, B // ODD - 1) as i:
                for odd in range(ODD):
                    step(ODD * i + odd, odd, i)
            for b in range(B - ODD, B):
                step(b, b % ODD, b // ODD, last=True)
            for half in range(2):
                join(B - 2, 0, B // ODD - 1, half)
            for g in range(G):
                evacuate_x4(B - 1, g)
            for half in range(2):
                join(B - 1, 1, B // ODD - 1, half)

        @block.vector
        def _(dve):
            dve.wait_ge(ident_ready, 1)
            nc.vector.tensor_reduce(in_rank[:, :], ident[:, :].rearrange("p (g c) -> p c g", g=G),
                                    AX.X, ALU.add).then_inc(masks_ready, 1)
            nc.vector.tensor_reduce(in_group[:, :], ident[:, :].rearrange("p (g c) -> p g c", g=G),
                                    AX.X, ALU.add).then_inc(masks_ready, 1)
            dve.wait_ge(masks_ready, 2)
            nc.vector.tensor_copy(spread_cq[:, :, :],
                                  in_rank[:, :].unsqueeze(2).broadcast_to([C, GROUP, PH])
                                  ).then_inc(masks_ready, 1)
            for l in range(2):
                nc.vector.tensor_copy(expert[l][:, K, :], ident[:, :]).then_inc(eye_ready, 1)
                nc.vector.memset(att[l][:, K:KI], 1.0).then_inc(eye_ready, 1)
            dve.wait_ge(s_in, ALL_LOADED)
            for l, to in enumerate((bias1, bias4_ch)):
                dve.wait_ge(ctx_done, l + 1)
                nc.vector.tensor_scalar(to[:, :], bank[6 + l][:, 0:B], side[:, :], None, ALU.add
                                        ).then_inc(ctx_ready, 1)
            dve.wait_ge(ctx_ready, 2)
            nc.vector.tensor_tensor(bias4_g, bias4_ch[:, :].unsqueeze(1).broadcast_to([C, G, B]),
                                    in_group[:, :].unsqueeze(2).broadcast_to([C, G, B]), ALU.mult
                                    ).then_inc(bias4_g_ready, 1)

            def low_x(b):
                dve.wait_ge(x_hi_ready, b + 1)
                nc.vector.tensor_tensor(x_lo[:, :, HALO:N + HALO], x_ph[:, :, :],
                                        x_hi[:, :, HALO:N + HALO].bitcast(f32), ALU.subtract
                                        ).then_inc(x_lo_ready, 1)

            def conv_weights(l):
                dve.wait_ge(taps_placed[l], DMA * PH * PH)
                middle = band[l][:, HALO, :, :, :].rearrange("r q g o -> r g o q")
                same = ident[:, :].rearrange("r (o q) -> r o q", q=PH)
                nc.vector.tensor_tensor(middle, middle,
                                        same.unsqueeze(1).broadcast_to([C, G, GROUP, PH]),
                                        ALU.add).then_inc(band_ready, 1)
                dve.wait_ge(band_ready, l + 1)
                for m in range(BLK):
                    whole = band[l][:, m, :, :, :].rearrange("r q g o -> r g o q")
                    hi, lo = (w[l][:, m, :, :].rearrange("r g (o q) -> r g o q", q=PH)
                              for w in (w_hi, w_lo))
                    nc.vector.tensor_copy(hi, whole).then_inc(w_hi_ready, 1)
                    dve.wait_ge(w_hi_ready, BLK * l + m + 1)
                    nc.vector.tensor_tensor(lo, whole, hi.bitcast(f32), ALU.subtract
                                            ).then_inc(w_lo_ready, 1)

            for l in range(2):
                dve.wait_ge(score_done, l + 1)
                nc.vector.tensor_reduce(top[l][:, :], bank[4 + l][0:B, 0:K], AX.X, ALU.max, negate=True
                                        ).then_inc(top_ready, 1)
            conv_weights(0)
            low_x(0)
            for l in range(2):
                dve.wait_ge(exp_ready, l + 1)
                nc.vector.reciprocal(share[l][:, :], total[l][:, :]).then_inc(share_ready, 1)
                dve.wait_ge(share_ready, l + 1)
                nc.vector.tensor_scalar(att[l][:, 0:K], att[l][:, 0:K], share[l][:, :], None, ALU.mult
                                        ).then_inc(att_ready, 1)
                dve.wait_ge(att_ready, l + 1)
                dve.wait_ge(eye_ready, 4)
                nc.vector.tensor_tensor(att_diag[l].rearrange("p (b k) -> p b k", k=KI),
                                        att[l][:, :].unsqueeze(1).broadcast_to([B, B, KI]),
                                        ident[0:B, 0:B].unsqueeze(2).broadcast_to([B, B, KI]), ALU.mult
                                        ).then_inc(diag_ready, 1)
            for l in range(2):
                dve.wait_ge(att_t_done, l + 1)
                nc.vector.tensor_copy(att_t[l][:, :], bank[l][0:K, 0:B]).then_inc(att_t_ready, 1)
            for l in range(2):
                for n in range(THIRDS):
                    dve.wait_ge(mix_done, THIRDS * l + n + 1)
                    nc.vector.tensor_copy(
                        mix[l][:, :, :].rearrange("p b k -> p (b k)")[:, n * THIRD:(n + 1) * THIRD],
                        bank[2 + n][:, 0:THIRD]).then_inc(mix_copied, 1)
            for l in range(2):
                dve.wait_ge(bias_l_done, l + 1)
                nc.vector.tensor_copy(bias_l[l][:, :], bank[l][:, 0:B]).then_inc(bias_l_ready, 1)
            dve.wait_ge(bias4_done, 1)
            nc.vector.tensor_copy(bias4[:, :, :].rearrange("p g b -> p (g b)"), bank[7][:, 0:G * B]
                                  ).then_inc(bias4_all, 1)
            dve.wait_ge(mix_copied, 2 * THIRDS)
            dve.wait_ge(bias4_all, 1)
            dve.wait_ge(bias_l_ready, 2)
            for l, (of, to) in enumerate(((bias1, carried), (carried, bias3))):
                dve.wait_ge(vec_done, l + 1)
                for h in range(2):
                    ks = slice(h * K // 2, (h + 1) * K // 2)
                    nc.vector.tensor_tensor(vec_part[:, :, ks], mix[l][:, :, ks],
                                            vec_ps[:, h, :].rearrange("p (k b) -> p b k", b=B),
                                            ALU.mult).then_inc(vec_weighted, 1)
                dve.wait_ge(vec_weighted, 2 * l + 2)
                nc.vector.tensor_reduce(to[:, :], vec_part, AX.X, ALU.add).then_inc(vec_summed, 1)
                dve.wait_ge(vec_summed, 3 * l + 1)
                nc.vector.tensor_tensor(to[:, :], to[:, :], of[:, :], ALU.add).then_inc(vec_summed, 1)
                dve.wait_ge(vec_summed, 3 * l + 2)
                nc.vector.tensor_tensor(to[:, :], to[:, :], bias_l[l][:, :], ALU.add
                                        ).then_inc(vec_summed, 1)
                dve.wait_ge(vec_summed, 3 * l + 3)

            def weight_experts(b, l):
                wait(dve, mix_ready, 2 * b + l)
                nc.vector.tensor_tensor(weighted[:, :, :], expert[l][:, :, :],
                                        mix[l][:, b, :].unsqueeze(2).broadcast_to([C, KI, C]),
                                        ALU.mult).then_inc(weighted_ready, 1)

            def sum_experts(b, l):
                dve.wait_ge(weighted_ready, 2 * b + l + 1)
                nc.vector.tensor_reduce(mixed[l][:, :], weighted[:, :, :].rearrange("p k c -> p c k"),
                                        AX.X, ALU.add).then_inc(mix_ready, 1)

            def copy_m(b):
                dve.wait_ge(m_done, b + 1)
                nc.vector.tensor_copy(m_t[:, :], m_ps).then_inc(m_ready, 1)

            def high_m(b):
                dve.wait_ge(m_ready, b + 1)
                nc.vector.tensor_copy(m_hi[:, :], m_t[:, :]).then_inc(m_split, 1)

            def low_m(b):
                dve.wait_ge(m_split, 2 * b + 1)
                nc.vector.tensor_tensor(m_lo[:, :], m_t[:, :], m_hi[:, :].bitcast(f32), ALU.subtract
                                        ).then_inc(m_split, 1)

            def set_bias3(b):
                wait(dve, x3_ready, 2 * b)
                nc.vector.tensor_scalar(bias3_now[:, :], bias3[:, bass.ds(b, 1)], 0.0, None, ALU.add
                                        ).then_inc(bias3_ready, 1)

            def split_x1(b):
                dve.wait_ge(x1_moved, DMA * G * (b + 1))
                for q in range(PH + 1):
                    if q < PH:
                        nc.vector.tensor_copy(x1_hi[:, q, :], x1_ch[:, q, :]).then_inc(x1_high, 1)
                    if q >= 1:
                        dve.wait_ge(x1_high, PH * b + q)
                        nc.vector.tensor_tensor(x1_lo[:, q - 1, :], x1_ch[:, q - 1, :],
                                                x1_hi[:, q - 1, :].bitcast(f32), ALU.subtract
                                                ).then_inc(x1_split, 1)

            def split_x3(b):
                for g in range(G + 1):
                    if g < G:
                        dve.wait_ge(x3_moved[g], DMA * (b + 1))
                        nc.vector.tensor_copy(x3_hi[:, g, HALO:N + HALO], x3_ph[:, g, :]
                                              ).then_inc(x3_high, 1)
                    if g >= 1:
                        dve.wait_ge(x3_high, G * b + g)
                        nc.vector.tensor_tensor(x3_lo[:, g - 1, HALO:N + HALO], x3_ph[:, g - 1, :],
                                                x3_hi[:, g - 1, HALO:N + HALO].bitcast(f32),
                                                ALU.subtract).then_inc(x3_split, 1)

            def set_bias4(b):
                wait(dve, x4_ready, G * b)
                nc.vector.tensor_scalar(bias4_now[:, :], bias4[:, :, b], 0.0, None, ALU.add
                                        ).then_inc(bias4_ready, 1)

            def step(b, first=False, last=False):
                copy_m(b)
                if not last:
                    weight_experts(b + 1, 0)
                high_m(b)
                if not last:
                    sum_experts(b + 1, 0)
                low_m(b)
                if not first:
                    split_x3(b - 1)
                if not last:
                    weight_experts(b + 1, 1)
                set_bias3(b)
                if not last:
                    sum_experts(b + 1, 1)
                split_x1(b)
                if not last:
                    low_x(b + 1)
                set_bias4(b)

            for l in range(2):
                weight_experts(0, l)
                sum_experts(0, l)
            conv_weights(1)
            step(0, first=True)
            with dve.Fori(1, B - 1) as b:
                step(b)
            step(B - 1, last=True)
            split_x3(B - 1)

        @block.tensor
        def _(pe):
            pe.wait_ge(s_in, ALL_LOADED)
            for l in range(2):
                nc.tensor.matmul(bank[l][:, 0:B], w0[l][:, :], cond_t[:, :], start=True, stop=True
                                 ).then_inc(h1_done, 1)
            for l in range(2):
                nc.tensor.matmul(bank[6 + l][:, 0:B], cw[l][:, :], cond_t[:, :], start=True, stop=True
                                 ).then_inc(ctx_done, 1)
            for l in range(2):
                pe.wait_ge(h1_ready, l + 1)
                nc.tensor.matmul(bank[2 + l][:, 0:B], w1[l][:, :], h1[l][:, :], start=True, stop=True
                                 ).then_inc(h2_done, 1)
            pe.wait_ge(ident_ready, 1)
            for l in range(2):
                pe.wait_ge(h2_ready, l + 1)
                nc.tensor.matmul(bank[4 + l][0:B, 0:K], h2[l][:, :], w2[l][:, :], start=True, stop=False)
                nc.tensor.matmul(bank[4 + l][0:B, 0:K], ones[0:1, 0:B], b2[l][:, :], start=False,
                                 stop=True).then_inc(score_done, 1)
            pe.wait_ge(bias4_g_ready, 1)
            pe.wait_ge(masks_ready, 3)
            nc.tensor.matmul(bank[7][:, 0:G * B], spread_cq[:, :, :].rearrange("p c q -> p (c q)"),
                             bias4_g.rearrange("p g b -> p (g b)"), start=True, stop=True
                             ).then_inc(bias4_done, 1)
            for l in range(2):
                pe.wait_ge(h1_ready, l + 1)
                pe.wait_ge(att_ready, l + 1)
                nc.tensor.transpose(bank[l][0:K, 0:B], att[l][:, 0:K], ident[0:B, 0:B]
                                    ).then_inc(att_t_done, 1)
            for l in range(2):
                pe.wait_ge(diag_ready, l + 1)
                for n in range(THIRDS):
                    if l == 0:
                        pe.wait_ge(exp_ready, 2)
                    else:
                        pe.wait_ge(mix_copied, n + 1)
                    nc.tensor.matmul(bank[2 + n][:, 0:THIRD], ones[0:B, :],
                                     att_diag[l][:, n * THIRD:(n + 1) * THIRD], start=True, stop=True
                                     ).then_inc(mix_done, 1)
            for l in range(2):
                pe.wait_ge(att_t_ready, l + 1)
                nc.tensor.matmul(bank[l][:, 0:B], bias_k[l][:, :], att_t[l][:, :], start=True,
                                 stop=True).then_inc(bias_l_done, 1)
            for l, (w, vector) in enumerate(((expert_t, bias1), (expert[1], carried))):
                pe.wait_ge(bias4_all, 1)
                wait(pe, vec_summed, 3 * l)
                for k in range(K):
                    mm = nc.tensor.matmul(vec_ps[:, k // (K // 2), k % (K // 2) * B:][:, 0:B],
                                          w[:, k, :], vector[:, :], start=True, stop=True)
                mm.then_inc(vec_done, 1)
            pe.wait_ge(mix_copied, 2 * THIRDS)
            pe.wait_ge(bias_l_ready, 2)
            pe.wait_ge(vec_weighted, 4)

            def conv(l, g, hi, lo, done):
                for m in range(BLK):
                    for w, x in ((w_hi, hi), (w_hi, lo), (w_lo, hi)):
                        mm = nc.tensor.matmul(conv_bank[g % 2], w[l][:, m, g, :], x[:, g, m:m + N],
                                              start=(m == 0 and x is hi and w is w_hi),
                                              stop=(m == BLK - 1 and w is w_lo))
                mm.then_inc(done, 1)

            def conv1(b):
                pe.wait_ge(x_lo_ready, b + 1)
                for g in range(G):
                    if g >= 2:
                        pe.wait_ge(x1_ready, G * b + g - 1)
                    elif isinstance(b, int) and b == 1:
                        pe.wait_ge(x1_ready, g + 3)
                    elif not isinstance(b, int) or b >= 2:
                        pe.wait_ge(x4_ready, G * (b - 2) + g + 3)
                    conv(0, g, x_hi, x_lo, conv1_done)

            def conv4(b, after_x4=False):
                for g in range(G):
                    pe.wait_ge(x3_split, G * b + g + 1)
                    if g >= 2:
                        pe.wait_ge(x4_ready, G * b + g - 1)
                    elif after_x4:
                        pe.wait_ge(x4_ready, G * (b - 1) + g + 3)
                    else:
                        pe.wait_ge(x1_ready, G * (b + 1) + g + 3)
                    conv(1, g, x3_hi, x3_lo, conv4_done)

            def middle_matrix(b):
                pe.wait_ge(mix_ready, 2 * b + 2)
                wait(pe, m_ready, b)
                nc.tensor.matmul(m_ps, mixed[0][:, :], mixed[1][:, :], start=True, stop=True
                                 ).then_inc(m_done, 1)

            def middle(b):
                wait(pe, x3_ready, 2 * b)
                pe.wait_ge(m_split, 2 * b + 2)
                for q in range(PH):
                    pe.wait_ge(x1_split, PH * b + q + 1)
                    for m, x in ((m_hi, x1_hi), (m_hi, x1_lo), (m_lo, x1_hi)):
                        mm = nc.tensor.matmul(mid_bank[:, q, :], m[:, :], x[:, q, :],
                                              start=(m is m_hi and x is x1_hi), stop=(m is m_lo))
                    mm.then_inc(mid_done, 1)

            def step(b):
                middle_matrix(b)
                conv1(b)
                if not isinstance(b, int) or b >= 1:
                    conv4(b - 1)
                middle(b)

            pe.wait_ge(w_lo_ready, BLK)
            step(0)
            pe.wait_ge(w_lo_ready, 2 * BLK)
            step(1)
            with pe.Fori(2, B) as b:
                step(b)
            conv4(B - 1, after_x4=True)


def kernel(**inputs):
    import numpy as np
    import concourse.bacc as bacc
    from concourse.bass_utils import run_bass_kernel_spmd

    def grouped(w):
        out_c, in_c, k = w.shape
        return w.reshape(out_c // in_c, in_c, in_c, k).transpose(2, 3, 0, 1).reshape(in_c, -1)

    v = {n: np.asarray(x) for n, x in inputs.items()}
    laid = {
        "x": v["x"], "cond_t": v["cond_128"].T, "side": v["fside_S_0"][:, None],
        "W0": grouped(v["L0_cond_weight"]), "W1": grouped(v["L3_cond_weight"]),
        "cw0": v["L0_cond_c_weight"].T, "cw1": v["L3_cond_c_weight"].T,
        "e0": v["L1_cond_weight"][..., 0], "e1": v["L2_cond_weight"][..., 0].transpose(0, 2, 1),
        "e0_t": v["L1_cond_weight"][..., 0].transpose(0, 2, 1),
    }
    for l in range(2):
        n = f"L{l + 1}_cond_"
        laid |= {f"w0_{l}": v[n + "W0"], f"w1_{l}": v[n + "W1"], f"w2_{l}": v[n + "W2"],
                 f"b0_{l}": v[n + "b0"][:, None], f"b1_{l}": v[n + "b1"][:, None],
                 f"b2_{l}": v[n + "b2"][None, :], f"bias_k{l}": v[n + "bias_k"]}
    nc = bacc.Bacc("TRN2", target_bir_lowering=False, num_devices=1)
    arrays, args = {}, {}
    for name, x in laid.items():
        x = np.ascontiguousarray(x)
        arrays[f"in_{name}"] = x
        args[name] = nc.dram_tensor(f"in_{name}", x.shape, mybir.dt.from_np(x.dtype),
                                    kind="ExternalInput").ap()
    out = nc.dram_tensor("out", v["x"].shape, mybir.dt.from_np(v["x"].dtype),
                         kind="ExternalOutput").ap()
    cond_resid_kernel(nc, args, out)
    return run_bass_kernel_spmd(nc, [arrays], core_ids=[0]).results[0]["out"]
```

```python
import concourse.bass as bass
from concourse import mybir
from contextlib import ExitStack


def cond_resid_kernel(nc: bass.Bass, a, out):
    f32, f32r = mybir.dt.float32, mybir.dt.float32r
    ALU, ACT, AX = mybir.AluOpType, mybir.ActivationFunctionType, mybir.AxisListType

    B, C, L = a["x"].shape
    GROUP = a["W0"].shape[0]
    TAPS = a["W0"].shape[1] // C
    G = C // GROUP
    PH = C // GROUP
    N = L // PH
    BLK = (PH + TAPS - 1) // PH
    HALO = BLK // 2
    K = a["e0"].shape[0]
    KI = K + 1
    DMA = 16
    ODD = 2

    ctx = ExitStack()
    with ctx:
        def sb(name, shape, dt=f32):
            return ctx.enter_context(nc.sbuf_tensor(name, shape, dt))

        def sem(name):
            return ctx.enter_context(nc.semaphore(name))

        x_in = sb("x_in", [C, ODD, L])
        x_ch = sb("x_ch", [C, PH, N])
        x_ph = sb("x_ph", [C, G, N])
        x_hi = sb("x_hi", [C, G, N + 2 * HALO], f32r)
        x_lo = sb("x_lo", [C, G, N + 2 * HALO], f32r)
        x1_ph = sb("x1_ph", [C, G, N])
        x1_ch = sb("x1_ch", [C, PH, N])
        x1_hi = sb("x1_hi", [C, PH, N], f32r)
        x1_lo = sb("x1_lo", [C, PH, N], f32r)
        x3_ch = sb("x3_ch", [C, PH, N])
        x3_ph = sb("x3_ph", [C, G, N])
        x3_hi = sb("x3_hi", [C, G, N + 2 * HALO], f32r)
        x3_lo = sb("x3_lo", [C, G, N + 2 * HALO], f32r)
        x4_ph = sb("x4_ph", [C, G, N])
        x4_ch = sb("x4_ch", [C, PH, N])
        x_out = sb("x_out", [C, ODD, L])
        band = [x_out[:, l, 0:BLK * PH * C].rearrange("r (j g o) -> r j g o", j=BLK * PH, g=G)
                for l in range(2)]
        w_hi = [sb(f"w_hi{l}", [C, BLK, G, C], f32r) for l in range(2)]
        w_lo = [sb(f"w_lo{l}", [C, BLK, G, C], f32r) for l in range(2)]
        expert = [sb(f"expert{l}", [C, KI, C]) for l in range(2)]
        mix = [sb(f"mix{l}", [C, B, KI]) for l in range(2)]
        weighted = sb("weighted", [C, KI, C])
        mixed = [sb(f"mixed{l}", [C, C]) for l in range(2)]
        m_t = sb("m_t", [C, C])
        m_hi = sb("m_hi", [C, C], f32r)
        m_lo = sb("m_lo", [C, C], f32r)
        bias1 = sb("bias1", [C, B])
        bias_l = [sb(f"bias_l{l}", [C, B]) for l in range(2)]
        bias4_ch = sb("bias4_ch", [C, B])
        bias4 = sb("bias4", [C, G, B])
        bias3 = sb("bias3", [C, B])
        carried = sb("carried", [C, B])
        bias3_now = sb("bias3_now", [C, 1])
        bias4_now = sb("bias4_now", [C, G])
        ident = sb("ident", [C, C])
        ones = sb("ones", [C, C])
        in_rank = sb("in_rank", [C, GROUP])
        spread_cq = sb("spread_cq", [C, GROUP, PH])
        in_group = sb("in_group", [C, G])
        b2 = sb("b2", [1, 2, K])
        bias_k = sb("bias_k", [K, 2, C])
        top = [sb(f"top{l}", [B, 1]) for l in range(2)]
        total = [sb(f"total{l}", [B, 1]) for l in range(2)]
        share = [sb(f"share{l}", [B, 1]) for l in range(2)]
        att = [sb(f"att{l}", [B, KI]) for l in range(2)]
        att_t = [sb(f"att_t{l}", [K, B]) for l in range(2)]
        att_diag = [t[0:B, :, :].rearrange("p g n -> p (g n)")[:, 0:B * KI] for t in (x1_ch, x4_ch)]
        expert_t = x3_ph[:, :, :].rearrange("p g n -> p (g n)")[:, 0:K * C].rearrange(
            "p (k c) -> p k c", k=K)
        vec_part = x3_ch[:, :, :].rearrange("p q n -> p (q n)")[:, 0:B * K].rearrange(
            "p (b k) -> p b k", k=K)
        spare = x3_ph[:, G // 2:, :].rearrange("p g n -> p (g n)")
        small = spare[:, 0:a["small"].shape[1]]
        columns = iter(range(small.shape[1]))

        def take(width):
            first = [next(columns) for _ in range(width)][0]
            return small[:, first:first + width]

        cond_t, side = take(B), take(1)
        w0, w1, cw, w2, b0, b1 = ([take(width) for l in range(2)] for width in (C, C, C, K, 1, 1))
        spare = x3_ch[:, PH // 2:, :].rearrange("p q n -> p (q n)")
        h1, h2 = ([spare[:, (2 * n + l) * B:(2 * n + l + 1) * B] for l in range(2)] for n in range(2))
        bias4_g = x4_ph[:, 0, 0:G * B].rearrange("p (g b) -> p g b", g=G)

        pair = [ctx.enter_context(nc.psum_tensor(f"pair{n}", [C, 2, N], f32)) for n in range(2)]
        quad = ctx.enter_context(nc.psum_tensor("quad", [C, PH, N], f32))
        bank = [pair[0][:, 0, :], pair[0][:, 1, :], *(quad[:, n, :] for n in range(PH)),
                pair[1][:, 0, :], pair[1][:, 1, :]]
        conv_bank = bank[0:2]
        mid_bank = quad
        m_ps = bank[6][:, 0:C]
        vec_ps = pair[1][:, :, 0:K // 2 * B]

        small_loaded = sem("small_operands_loaded")
        rows_loaded = sem("b2_and_bias_k_loaded")
        experts_loaded = sem("experts_loaded")
        expert_t_loaded = sem("transposed_experts_loaded")
        taps_placed = [sem(f"conv_taps_placed{l}") for l in range(2)]
        zeroed = sem("ident_ones_halos_filled")
        ident_ready = sem("identity_ready")
        h1_done = sem("hidden1_in_psum")
        h1_ready = sem("hidden1_in_sbuf")
        h2_done = sem("hidden2_in_psum")
        h2_ready = sem("hidden2_in_sbuf")
        score_done = sem("scores_in_psum")
        top_ready = sem("score_maximum_negated")
        exp_ready = sem("exponentials_ready")
        share_ready = sem("one_over_their_sum")
        att_ready = sem("attention_ready")
        diag_ready = sem("attention_on_diagonal")
        att_t_done = sem("attention_transposed_in_psum")
        att_t_ready = sem("attention_transposed_in_sbuf")
        mix_done = sem("mix_third_in_psum")
        mix_copied = sem("mix_third_in_sbuf")
        bias_l_done = sem("layer_bias_in_psum")
        bias_l_ready = sem("layer_bias_in_sbuf")
        ctx_done = sem("context_in_psum")
        ctx_ready = sem("context_bias_in_sbuf")
        masks_ready = sem("spread_and_group_masks")
        bias4_g_ready = sem("bias4_masked_by_group")
        bias4_done = sem("bias4_in_psum")
        bias4_all = sem("bias4_in_sbuf")
        vec_done = sem("expert_vectors_in_psum")
        vec_weighted = sem("expert_vectors_weighted")
        vec_summed = sem("expert_vectors_summed")
        eye_ready = sem("identity_expert_written")
        band_zeroed = sem("band_zeroed")
        band_ready = sem("band_with_residual")
        w_hi_ready = sem("conv_weights_high")
        w_lo_ready = sem("conv_weights_low")
        weighted_ready = sem("experts_weighted")
        x_loaded = [sem(f"x_loaded{n}") for n in range(ODD)]
        x_cut = sem("x_half_cut_in_phases")
        x_moved = sem("x_moved_to_phase_rows")
        x_hi_ready = sem("x_high_ready")
        x_lo_ready = sem("x_low_ready")
        conv1_done = sem("conv1_group_done")
        x1_ready = sem("x1_group_evacuated")
        x1_moved = sem("x1_moved_to_channel_rows")
        mix_ready = sem("mixed_matrices_ready")
        m_done = sem("middle_matrix_in_psum")
        m_ready = sem("middle_matrix_in_sbuf")
        m_split = sem("middle_matrix_split")
        bias3_ready = sem("x3_bias_ready")
        x1_high = sem("x1_phase_high_ready")
        x1_split = sem("x1_phase_split")
        mid_done = sem("middle_phase_done")
        x3_ready = sem("x3_half_evacuated")
        x3_moved = [sem(f"x3_group{g}_moved_to_phase_rows") for g in range(G)]
        x3_high = sem("x3_group_high_ready")
        x3_split = sem("x3_group_split")
        bias4_ready = sem("bias4_ready")
        conv4_done = sem("conv4_group_done")
        x4_ready = sem("x4_group_evacuated")
        x4_moved = sem("x4_moved_to_channel_rows")
        x_joined = sem("x_out_half_joined")
        x_stored = [sem(f"x_stored{n}") for n in range(ODD)]

        ALL_ZEROED = 2 + 4 * 2
        THIRDS = 3
        THIRD = B * KI // THIRDS

        def wait(eng, s, value):
            if not (isinstance(value, int) and value <= 0):
                eng.wait_ge(s, value)

        block = ctx.enter_context(nc.Block())

        @block.sync
        def _(sp):
            def load(b, slot):
                sp.dma_start(x_in[:, slot, :], a["x"][b, :, :]).then_inc(x_loaded[slot], DMA)

            def move_x(b):
                for g in range(G):
                    sp.dma_start(x_ph[:, g, :], x_ch[GROUP * g:GROUP * (g + 1), :, :]
                                 ).then_inc(x_moved, DMA)

            def move_x1(b, g):
                sp.wait_ge(x1_ready, G * b + g + 1)
                sp.dma_start(x1_ch[GROUP * g:GROUP * (g + 1), :, :], x1_ph[:, g, :]
                             ).then_inc(x1_moved, DMA)

            def move_x4(b, g):
                if g == 0:
                    wait(sp, x_joined, 2 * b)
                sp.wait_ge(x4_ready, G * b + g + 1)
                sp.dma_start(x4_ch[GROUP * g:GROUP * (g + 1), :, :], x4_ph[:, g, :]
                             ).then_inc(x4_moved, DMA)

            def store(b, slot):
                sp.dma_start(out[b, :, :], x_out[:, slot, :]).then_inc(x_stored[slot], DMA)

            def move_x3(b):
                sp.wait_ge(x3_ready, 2 * b + 2)
                for g in range(G):
                    sp.dma_start(x3_ph[:, g, :], x3_ch[GROUP * g:GROUP * (g + 1), :, :]
                                 ).then_inc(x3_moved[g], DMA)

            def step(b, slot, whole=True):
                if whole or b >= 1:
                    move_x3(b - 1)
                move_x1(b, 0)
                if whole or b + 1 < B:
                    move_x(b + 1)
                for g in range(1, G):
                    move_x1(b, g)
                if whole or b + 3 < B:
                    load(b + 3, (slot + 3) % ODD)
                for g in range(G):
                    if g == G - 1 and (whole or b >= 2):
                        store(b - 2, slot)
                    if whole or b >= 1:
                        move_x4(b - 1, g)

            def place_taps(l):
                sp.wait_ge(band_zeroed, l + 1)
                taps = a[f"W{l}"].rearrange("c (k g o) -> c k g o", k=TAPS, g=G)
                for p in range(PH):
                    rows, first = slice(p, PH * (GROUP - 1) + p + 1, PH), PH - 1 - p
                    sp.dma_start(band[l][rows, first:first + TAPS, :, :], taps
                                 ).then_inc(taps_placed[l], DMA)

            load(0, 0)
            place_taps(0)
            sp.wait_ge(x_cut, 2)
            move_x(0)
            sp.dma_start(expert_t, a["e0_t"].rearrange("k r c -> r k c")).then_inc(expert_t_loaded, DMA)
            load(1, 1)
            place_taps(1)
            load(2, 0)
            for b in range(2):
                step(b, b, whole=False)
            with sp.Fori(1, (B - 4) // 2) as i:
                for odd in range(ODD):
                    step(2 * i + odd, odd)
            for b in range(B - 4, B):
                step(b, b % ODD, whole=False)
            move_x3(B - 1)
            move_x4(B - 1, 0)
            store(B - 2, 0)
            for g in range(1, G):
                move_x4(B - 1, g)
            sp.wait_ge(x_joined, 2 * B)
            store(B - 1, 1)
            for slot in range(ODD):
                sp.wait_ge(x_stored[slot], DMA * B // ODD)

        @block.gpsimd
        def _(pool):
            pool.memset(band[0][:, :, :, :], 0.0).then_inc(band_zeroed, 1)
            pool.memset(ident[:, :], 0.0).then_inc(zeroed, 1)
            pool.memset(ones[:, :], 1.0).then_inc(zeroed, 1)
            for h in (x_hi, x_lo, x3_hi, x3_lo):
                for edge in (h[:, :, 0:HALO], h[:, :, N + HALO:N + 2 * HALO]):
                    pool.memset(edge.bitcast(f32), 0.0).then_inc(zeroed, 1)
            pool.wait_ge(zeroed, ALL_ZEROED)
            pool.affine_select(out=ident[:, :], in_=ident[:, :], compare_op=ALU.not_equal, fill=1.0,
                               base=0, pattern=[[-1, C]], channel_multiplier=1
                               ).then_inc(ident_ready, 1)
            pool.memset(band[1][:, :, :, :], 0.0).then_inc(band_zeroed, 1)

        @block.scalar
        def _(act):
            def cut(b, slot, turn, half):
                if half == 0:
                    act.wait_ge(x_loaded[slot], DMA * (turn + 1))
                    wait(act, x_moved, DMA * G * b)
                phases = slice(half * PH // 2, (half + 1) * PH // 2)
                nc.scalar.copy(x_ch[:, phases, :],
                               x_in[:, slot, :].rearrange("c (n p) -> c p n", p=PH)[:, phases, :]
                               ).then_inc(x_cut, 1)

            def round_x(b):
                act.wait_ge(x_moved, DMA * G * (b + 1))
                wait(act, conv1_done, G * b)
                nc.scalar.copy(x_hi[:, :, HALO:N + HALO], x_ph[:, :, :]).then_inc(x_hi_ready, 1)

            act.dma_start(small, a["small"]).then_inc(small_loaded, DMA)
            act.dma_start(b2[:, :, :], a["b2"]).then_inc(rows_loaded, DMA)
            act.dma_start(bias_k[:, :, :], a["bias_k"]).then_inc(rows_loaded, DMA)
            for l in range(2):
                act.dma_start(expert[l][:, 0:K, :], a[f"e{l}"].rearrange("k r c -> r k c")
                              ).then_inc(experts_loaded, DMA)
            for half in range(2):
                cut(0, 0, 0, half)
            act.wait_ge(small_loaded, DMA)
            for l in range(2):
                act.wait_ge(h1_done, l + 1)
                nc.scalar.activation(h1[l][:, :], bank[l][:, 0:B], ACT.Gelu, bias=b0[l][:, :]
                                     ).then_inc(h1_ready, 1)
            for l in range(2):
                act.wait_ge(h2_done, l + 1)
                nc.scalar.activation(h2[l][:, :], bank[2 + l][:, 0:B], ACT.Gelu, bias=b1[l][:, :]
                                     ).then_inc(h2_ready, 1)
            for l in range(2):
                act.wait_ge(top_ready, l + 1)
                nc.scalar.activation(att[l][:, 0:K], bank[4 + l][0:B, 0:K], ACT.Exp, bias=top[l][:, :],
                                     accum_out=total[l][:, :]).then_inc(exp_ready, 1)
            act.wait_ge(bias4_done, 1)
            nc.scalar.copy(bias4[:, :, :].rearrange("p g b -> p (g b)"), bank[7][:, 0:G * B]
                           ).then_inc(bias4_all, 1)
            round_x(0)
            for l in range(2):
                for n in range(THIRDS):
                    act.wait_ge(mix_done, THIRDS * l + n + 1)
                    nc.scalar.copy(
                        mix[l][:, :, :].rearrange("p b k -> p (b k)")[:, n * THIRD:(n + 1) * THIRD],
                        bank[2 + n][:, 0:THIRD]).then_inc(mix_copied, 1)
            for l in range(2):
                act.wait_ge(bias_l_done, l + 1)
                nc.scalar.copy(bias_l[l][:, :], bank[l][:, 0:B]).then_inc(bias_l_ready, 1)

            def join(b, slot, turn, half):
                if half == 0:
                    act.wait_ge(x4_moved, DMA * G * (b + 1))
                    wait(act, x_stored[slot], DMA * turn)
                phases = slice(half * PH // 2, (half + 1) * PH // 2)
                nc.scalar.copy(x_out[:, slot, :].rearrange("c (n p) -> c p n", p=PH)[:, phases, :],
                               x4_ch[:, phases, :]).then_inc(x_joined, 1)

            def evacuate_x1(b, g):
                if g == 0:
                    wait(act, x1_moved, DMA * G * b)
                act.wait_ge(conv1_done, G * b + g + 1)
                nc.scalar.copy(x1_ph[:, g, :], conv_bank[g % 2]).then_inc(x1_ready, 1)

            def evacuate_x4(b, g):
                if g == 0:
                    act.wait_ge(bias4_ready, b + 1)
                    wait(act, x4_moved, DMA * G * b)
                act.wait_ge(conv4_done, G * b + g + 1)
                nc.scalar.activation(x4_ph[:, g, :], conv_bank[g % 2], ACT.Identity,
                                     bias=bias4_now[:, g:g + 1]).then_inc(x4_ready, 1)

            def evacuate_x3(b):
                act.wait_ge(bias3_ready, b + 1)
                for half in range(2):
                    act.wait_ge(mid_done, PH * b + PH // 2 * (half + 1))
                    phases = slice(half * PH // 2, (half + 1) * PH // 2)
                    nc.scalar.activation(x3_ch[:, phases, :], mid_bank[:, phases, :], ACT.Identity,
                                         bias=bias3_now[:, :]).then_inc(x3_ready, 1)

            def step(b, slot, turn, first=False, last=False):
                evacuate_x1(b, 0)
                if not first:
                    join(b - 2, slot, turn - 1, 0)
                evacuate_x1(b, 1)
                if not first:
                    join(b - 2, slot, turn - 1, 1)
                evacuate_x1(b, 2)
                evacuate_x1(b, 3)
                for g in range(G):
                    if not (isinstance(b, int) and b == 0):
                        evacuate_x4(b - 1, g)
                    if g == 0 and not (last and slot == 1):
                        round_x(b + 1)
                    if not last and g in (1, 2):
                        cut(b + 2, slot, turn + 1, g - 1)
                evacuate_x3(b)

            for half in range(2):
                cut(1, 1, 0, half)
            for b in range(2 * ODD):
                step(b, b % ODD, b // ODD, first=(b < 2))
                if b == 1:
                    act.wait_ge(w_lo_ready, 2 * PH)
            with act.Fori(2, B // ODD - 1) as i:
                for odd in range(ODD):
                    step(ODD * i + odd, odd, i)
            for b in range(B - ODD, B):
                step(b, b % ODD, b // ODD, last=True)
            for half in range(2):
                join(B - 2, 0, B // ODD - 1, half)
            for g in range(G):
                evacuate_x4(B - 1, g)
            for half in range(2):
                join(B - 1, 1, B // ODD - 1, half)

        @block.vector
        def _(dve):
            dve.wait_ge(ident_ready, 1)
            nc.vector.tensor_reduce(in_rank[:, :], ident[:, :].rearrange("p (g c) -> p c g", g=G),
                                    AX.X, ALU.add).then_inc(masks_ready, 1)
            nc.vector.tensor_reduce(in_group[:, :], ident[:, :].rearrange("p (g c) -> p g c", g=G),
                                    AX.X, ALU.add).then_inc(masks_ready, 1)
            dve.wait_ge(masks_ready, 2)
            nc.vector.tensor_copy(spread_cq[:, :, :],
                                  in_rank[:, :].unsqueeze(2).broadcast_to([C, GROUP, PH])
                                  ).then_inc(masks_ready, 1)
            for l in range(2):
                nc.vector.tensor_copy(expert[l][:, K, :], ident[:, :]).then_inc(eye_ready, 1)
                nc.vector.memset(att[l][:, K:KI], 1.0).then_inc(eye_ready, 1)
            dve.wait_ge(small_loaded, DMA)
            for l, to in enumerate((bias1, bias4_ch)):
                dve.wait_ge(ctx_done, l + 1)
                nc.vector.tensor_scalar(to[:, :], bank[6 + l][:, 0:B], side[:, :], None, ALU.add
                                        ).then_inc(ctx_ready, 1)
            dve.wait_ge(ctx_ready, 2)
            nc.vector.tensor_tensor(bias4_g, bias4_ch[:, :].unsqueeze(1).broadcast_to([C, G, B]),
                                    in_group[:, :].unsqueeze(2).broadcast_to([C, G, B]), ALU.mult
                                    ).then_inc(bias4_g_ready, 1)

            def low_x(b):
                dve.wait_ge(x_hi_ready, b + 1)
                nc.vector.tensor_tensor(x_lo[:, :, HALO:N + HALO], x_ph[:, :, :],
                                        x_hi[:, :, HALO:N + HALO].bitcast(f32), ALU.subtract
                                        ).then_inc(x_lo_ready, 1)

            def add_residual(l):
                dve.wait_ge(taps_placed[l], DMA * PH)
                for q in range(PH):
                    column = band[l][:, PH * HALO + PH - 1 - q, :, :]
                    same = ident[:, :].rearrange("r (o q) -> r q o", q=PH)[:, q, :]
                    nc.vector.tensor_tensor(column, column,
                                            same.unsqueeze(1).broadcast_to([C, G, GROUP]), ALU.add
                                            ).then_inc(band_ready, 1)

            def columns_of(l, q):
                return (band[l][:, PH - 1 - q:PH * (BLK - 1) + PH - q:PH, :, :],
                        *(w[l][:, :, :, :].rearrange("r m g (o q) -> r q m g o", q=PH)[:, q]
                          for w in (w_hi, w_lo)))

            def high_weights(l):
                dve.wait_ge(band_ready, PH * (l + 1))
                for q in range(PH):
                    whole, high, _ = columns_of(l, q)
                    nc.vector.tensor_copy(high, whole).then_inc(w_hi_ready, 1)

            def low_weights(l):
                dve.wait_ge(w_hi_ready, PH * (l + 1))
                for q in range(PH):
                    whole, high, low = columns_of(l, q)
                    nc.vector.tensor_tensor(low, whole, high.bitcast(f32), ALU.subtract
                                            ).then_inc(w_lo_ready, 1)

            add_residual(0)
            for l in range(2):
                dve.wait_ge(score_done, l + 1)
                nc.vector.tensor_reduce(top[l][:, :], bank[4 + l][0:B, 0:K], AX.X, ALU.max, negate=True
                                        ).then_inc(top_ready, 1)
            high_weights(0)
            for l in range(2):
                dve.wait_ge(exp_ready, l + 1)
                nc.vector.reciprocal(share[l][:, :], total[l][:, :]).then_inc(share_ready, 1)
                dve.wait_ge(share_ready, l + 1)
                nc.vector.tensor_scalar(att[l][:, 0:K], att[l][:, 0:K], share[l][:, :], None, ALU.mult
                                        ).then_inc(att_ready, 1)
                dve.wait_ge(att_ready, l + 1)
                dve.wait_ge(eye_ready, 4)
                nc.vector.tensor_tensor(att_diag[l].rearrange("p (b k) -> p b k", k=KI),
                                        att[l][:, :].unsqueeze(1).broadcast_to([B, B, KI]),
                                        ident[0:B, 0:B].unsqueeze(2).broadcast_to([B, B, KI]), ALU.mult
                                        ).then_inc(diag_ready, 1)
            low_weights(0)
            for l in range(2):
                dve.wait_ge(att_t_done, l + 1)
                nc.vector.tensor_copy(att_t[l][:, :], bank[l][0:K, 0:B]).then_inc(att_t_ready, 1)

            def carry_bias(l):
                of, to = ((bias1, carried), (carried, bias3))[l]
                dve.wait_ge(vec_done, l + 1)
                for h in range(2):
                    ks = slice(h * K // 2, (h + 1) * K // 2)
                    nc.vector.tensor_tensor(vec_part[:, :, ks], mix[l][:, :, ks],
                                            vec_ps[:, h, :].rearrange("p (k b) -> p b k", b=B),
                                            ALU.mult).then_inc(vec_weighted, 1)
                dve.wait_ge(vec_weighted, 2 * l + 2)
                nc.vector.tensor_reduce(to[:, :], vec_part, AX.X, ALU.add).then_inc(vec_summed, 1)
                dve.wait_ge(vec_summed, 3 * l + 1)
                nc.vector.tensor_tensor(to[:, :], to[:, :], of[:, :], ALU.add).then_inc(vec_summed, 1)
                dve.wait_ge(vec_summed, 3 * l + 2)
                nc.vector.tensor_tensor(to[:, :], to[:, :], bias_l[l][:, :], ALU.add
                                        ).then_inc(vec_summed, 1)

            def weight_experts(b, l):
                wait(dve, mix_ready, 2 * b + l)
                nc.vector.tensor_tensor(weighted[:, :, :], expert[l][:, :, :],
                                        mix[l][:, b, :].unsqueeze(2).broadcast_to([C, KI, C]),
                                        ALU.mult).then_inc(weighted_ready, 1)

            def sum_experts(b, l):
                dve.wait_ge(weighted_ready, 2 * b + l + 1)
                nc.vector.tensor_reduce(mixed[l][:, :], weighted[:, :, :].rearrange("p k c -> p c k"),
                                        AX.X, ALU.add).then_inc(mix_ready, 1)

            def copy_m(b):
                dve.wait_ge(m_done, b + 1)
                nc.vector.tensor_copy(m_t[:, :], m_ps).then_inc(m_ready, 1)

            def high_m(b):
                dve.wait_ge(m_ready, b + 1)
                nc.vector.tensor_copy(m_hi[:, :], m_t[:, :]).then_inc(m_split, 1)

            def low_m(b):
                dve.wait_ge(m_split, 2 * b + 1)
                nc.vector.tensor_tensor(m_lo[:, :], m_t[:, :], m_hi[:, :].bitcast(f32), ALU.subtract
                                        ).then_inc(m_split, 1)

            def set_bias3(b):
                if isinstance(b, int) and b == 0:
                    dve.wait_ge(vec_summed, 6)
                wait(dve, x3_ready, 2 * b)
                nc.vector.tensor_scalar(bias3_now[:, :], bias3[:, bass.ds(b, 1)], 0.0, None, ALU.add
                                        ).then_inc(bias3_ready, 1)

            def split_x1(b):
                dve.wait_ge(x1_moved, DMA * G * (b + 1))
                for q in range(PH + 1):
                    if q < PH:
                        nc.vector.tensor_copy(x1_hi[:, q, :], x1_ch[:, q, :]).then_inc(x1_high, 1)
                    if q >= 1:
                        dve.wait_ge(x1_high, PH * b + q)
                        nc.vector.tensor_tensor(x1_lo[:, q - 1, :], x1_ch[:, q - 1, :],
                                                x1_hi[:, q - 1, :].bitcast(f32), ALU.subtract
                                                ).then_inc(x1_split, 1)

            def split_x3(b):
                for g in range(G + 1):
                    if g < G:
                        dve.wait_ge(x3_moved[g], DMA * (b + 1))
                        nc.vector.tensor_copy(x3_hi[:, g, HALO:N + HALO], x3_ph[:, g, :]
                                              ).then_inc(x3_high, 1)
                    if g >= 1:
                        dve.wait_ge(x3_high, G * b + g)
                        nc.vector.tensor_tensor(x3_lo[:, g - 1, HALO:N + HALO], x3_ph[:, g - 1, :],
                                                x3_hi[:, g - 1, HALO:N + HALO].bitcast(f32),
                                                ALU.subtract).then_inc(x3_split, 1)

            def set_bias4(b):
                wait(dve, x4_ready, G * b)
                nc.vector.tensor_scalar(bias4_now[:, :], bias4[:, :, b], 0.0, None, ALU.add
                                        ).then_inc(bias4_ready, 1)

            def step(b, last=False):
                copy_m(b)
                if not last:
                    weight_experts(b + 1, 0)
                high_m(b)
                if not last:
                    sum_experts(b + 1, 0)
                low_m(b)
                split_x3(b - 1)
                if not last:
                    weight_experts(b + 1, 1)
                set_bias3(b)
                if not last:
                    sum_experts(b + 1, 1)
                split_x1(b)
                if not last:
                    low_x(b + 1)
                set_bias4(b)

            low_x(0)
            dve.wait_ge(mix_copied, 2 * THIRDS)
            dve.wait_ge(bias4_all, 1)
            dve.wait_ge(bias_l_ready, 2)
            dve.wait_ge(experts_loaded, 2 * DMA)
            weight_experts(0, 0)
            carry_bias(0)
            sum_experts(0, 0)
            weight_experts(0, 1)
            sum_experts(0, 1)
            carry_bias(1)
            copy_m(0)
            weight_experts(1, 0)
            high_m(0)
            sum_experts(1, 0)
            low_m(0)
            weight_experts(1, 1)
            sum_experts(1, 1)
            set_bias3(0)
            split_x1(0)
            low_x(1)
            add_residual(1)
            high_weights(1)
            low_weights(1)
            set_bias4(0)
            with dve.Fori(1, B - 1) as b:
                step(b)
            step(B - 1, last=True)
            split_x3(B - 1)

        @block.tensor
        def _(pe):
            pe.wait_ge(small_loaded, DMA)
            for l in range(2):
                nc.tensor.matmul(bank[l][:, 0:B], w0[l][:, :], cond_t[:, :], start=True, stop=True
                                 ).then_inc(h1_done, 1)
            for l in range(2):
                nc.tensor.matmul(bank[6 + l][:, 0:B], cw[l][:, :], cond_t[:, :], start=True, stop=True
                                 ).then_inc(ctx_done, 1)
            for l in range(2):
                pe.wait_ge(h1_ready, l + 1)
                nc.tensor.matmul(bank[2 + l][:, 0:B], w1[l][:, :], h1[l][:, :], start=True, stop=True
                                 ).then_inc(h2_done, 1)
            pe.wait_ge(ident_ready, 1)
            pe.wait_ge(rows_loaded, 2 * DMA)
            for l in range(2):
                pe.wait_ge(h2_ready, l + 1)
                nc.tensor.matmul(bank[4 + l][0:B, 0:K], h2[l][:, :], w2[l][:, :], start=True, stop=False)
                nc.tensor.matmul(bank[4 + l][0:B, 0:K], ones[0:1, 0:B], b2[:, l, :], start=False,
                                 stop=True).then_inc(score_done, 1)
            pe.wait_ge(bias4_g_ready, 1)
            pe.wait_ge(masks_ready, 3)
            nc.tensor.matmul(bank[7][:, 0:G * B], spread_cq[:, :, :].rearrange("p c q -> p (c q)"),
                             bias4_g.rearrange("p g b -> p (g b)"), start=True, stop=True
                             ).then_inc(bias4_done, 1)
            for l in range(2):
                pe.wait_ge(h1_ready, l + 1)
                pe.wait_ge(att_ready, l + 1)
                nc.tensor.transpose(bank[l][0:K, 0:B], att[l][:, 0:K], ident[0:B, 0:B]
                                    ).then_inc(att_t_done, 1)
            for l in range(2):
                pe.wait_ge(diag_ready, l + 1)
                for n in range(THIRDS):
                    if l == 0:
                        pe.wait_ge(exp_ready, 2)
                    else:
                        pe.wait_ge(mix_copied, n + 1)
                    nc.tensor.matmul(bank[2 + n][:, 0:THIRD], ones[0:B, :],
                                     att_diag[l][:, n * THIRD:(n + 1) * THIRD], start=True, stop=True
                                     ).then_inc(mix_done, 1)
            for l in range(2):
                pe.wait_ge(att_t_ready, l + 1)
                nc.tensor.matmul(bank[l][:, 0:B], bias_k[:, l, :], att_t[l][:, :], start=True,
                                 stop=True).then_inc(bias_l_done, 1)

            def expert_vectors(l):
                w, vector = ((expert_t, bias1), (expert[1], carried))[l]
                for k in range(K):
                    mm = nc.tensor.matmul(vec_ps[:, k // (K // 2), k % (K // 2) * B:][:, 0:B],
                                          w[:, k, :], vector[:, :], start=True, stop=True)
                mm.then_inc(vec_done, 1)

            def conv(l, g, hi, lo, done):
                for m in range(BLK):
                    for w, x in ((w_hi, hi), (w_hi, lo), (w_lo, hi)):
                        mm = nc.tensor.matmul(conv_bank[g % 2], w[l][:, m, g, :], x[:, g, m:m + N],
                                              start=(m == 0 and x is hi and w is w_hi),
                                              stop=(m == BLK - 1 and w is w_lo))
                mm.then_inc(done, 1)

            def conv1(b, groups=range(G)):
                pe.wait_ge(x_lo_ready, b + 1)
                for g in groups:
                    if g >= 2:
                        pe.wait_ge(x1_ready, G * b + g - 1)
                    elif isinstance(b, int) and b == 1:
                        pe.wait_ge(x1_ready, g + 3)
                    elif not isinstance(b, int) or b >= 2:
                        pe.wait_ge(x4_ready, G * (b - 2) + g + 3)
                    conv(0, g, x_hi, x_lo, conv1_done)

            def conv4(b, after_x4=False):
                for g in range(G):
                    pe.wait_ge(x3_split, G * b + g + 1)
                    if g >= 2:
                        pe.wait_ge(x4_ready, G * b + g - 1)
                    elif after_x4:
                        pe.wait_ge(x4_ready, G * (b - 1) + g + 3)
                    else:
                        pe.wait_ge(x1_ready, G * (b + 1) + g + 3)
                    conv(1, g, x3_hi, x3_lo, conv4_done)

            def middle_matrix(b):
                pe.wait_ge(mix_ready, 2 * b + 2)
                wait(pe, m_ready, b)
                nc.tensor.matmul(m_ps, mixed[0][:, :], mixed[1][:, :], start=True, stop=True
                                 ).then_inc(m_done, 1)

            def middle(b):
                wait(pe, x3_ready, 2 * b)
                pe.wait_ge(m_split, 2 * b + 2)
                for q in range(PH):
                    pe.wait_ge(x1_split, PH * b + q + 1)
                    for m, x in ((m_hi, x1_hi), (m_hi, x1_lo), (m_lo, x1_hi)):
                        mm = nc.tensor.matmul(mid_bank[:, q, :], m[:, :], x[:, q, :],
                                              start=(m is m_hi and x is x1_hi), stop=(m is m_lo))
                    mm.then_inc(mid_done, 1)

            def step(b):
                middle_matrix(b)
                conv1(b)
                conv4(b - 1)
                middle(b)

            pe.wait_ge(bias4_all, 1)
            pe.wait_ge(expert_t_loaded, DMA)
            expert_vectors(0)
            pe.wait_ge(bias_l_ready, 2)
            pe.wait_ge(w_lo_ready, PH)
            conv1(0, range(G // 2))
            pe.wait_ge(vec_summed, 3)
            pe.wait_ge(experts_loaded, 2 * DMA)
            expert_vectors(1)
            conv1(0, range(G // 2, G))
            pe.wait_ge(vec_weighted, 4)
            middle_matrix(0)
            pe.wait_ge(mix_copied, 2 * THIRDS)
            middle(0)
            middle_matrix(1)
            conv1(1)
            pe.wait_ge(w_lo_ready, 2 * PH)
            conv4(0)
            middle(1)
            with pe.Fori(2, B) as b:
                step(b)
            conv4(B - 1, after_x4=True)


def kernel(**inputs):
    import numpy as np
    import concourse.bacc as bacc
    from concourse.bass_utils import run_bass_kernel_spmd

    def grouped(w):
        out_c, in_c, k = w.shape
        return w.reshape(out_c // in_c, in_c, in_c, k).transpose(2, 3, 0, 1).reshape(in_c, -1)

    v = {n: np.asarray(x) for n, x in inputs.items()}
    laid = {
        "x": v["x"],
        "W0": grouped(v["L0_cond_weight"]), "W1": grouped(v["L3_cond_weight"]),
        "e0": v["L1_cond_weight"][..., 0], "e1": v["L2_cond_weight"][..., 0].transpose(0, 2, 1),
        "e0_t": v["L1_cond_weight"][..., 0].transpose(0, 2, 1),
    }
    middle = [f"L{l + 1}_cond_" for l in range(2)]
    laid["small"] = np.concatenate(
        [v["cond_128"].T, v["fside_S_0"][:, None], *(v[n + "W0"] for n in middle),
         *(v[n + "W1"] for n in middle), v["L0_cond_c_weight"].T, v["L3_cond_c_weight"].T,
         *(v[n + "W2"] for n in middle), *(v[n + "b0"][:, None] for n in middle),
         *(v[n + "b1"][:, None] for n in middle)], axis=1)
    laid["b2"] = np.stack([v[n + "b2"] for n in middle])[None]
    laid["bias_k"] = np.stack([v[n + "bias_k"] for n in middle], axis=1)
    nc = bacc.Bacc("TRN2", target_bir_lowering=False, num_devices=1)
    arrays, args = {}, {}
    for name, x in laid.items():
        x = np.ascontiguousarray(x)
        arrays[f"in_{name}"] = x
        args[name] = nc.dram_tensor(f"in_{name}", x.shape, mybir.dt.from_np(x.dtype),
                                    kind="ExternalInput").ap()
    out = nc.dram_tensor("out", v["x"].shape, mybir.dt.from_np(v["x"].dtype),
                         kind="ExternalOutput").ap()
    cond_resid_kernel(nc, args, out)
    return run_bass_kernel_spmd(nc, [arrays], core_ids=[0]).results[0]["out"]
```
